# Optimizing a Trainium2 kernel written in Bass

```python
import numpy as np
import jax
import jax.numpy as jnp

def _softmax(x, axis=-1):
    return jax.nn.softmax(x, axis=axis)

def _gelu(x):
    return jax.nn.gelu(x, approximate=True)

def _silu(x):
    return jax.nn.silu(x)

def _sigmoid(x):
    return jax.nn.sigmoid(x)

def _layernorm(x, axis=-1, eps=1e-05):
    m = jnp.mean(x, axis=axis, keepdims=True)
    v = jnp.var(x, axis=axis, keepdims=True)
    return (x - m) / jnp.sqrt(v + eps)

def _scatter_add(tgt, idx, src, axis=0):
    return tgt.at[idx].add(src)

def _segment_sum(src, seg, n):
    return jax.ops.segment_sum(src, seg, n)
kernel_name = 'mk_adj_preln_d2_adj_r2_2fbaab'

def setup_inputs(seed: int=0):
    np.random.seed(seed)
    _w = jnp.asarray

    def _rec_inputs():
        import jax
        import jax.numpy as jnp
        _gk = jax.random.key(seed)
        x = -0.0005207 + 1.001 * jax.random.normal(jax.random.fold_in(_gk, 1), (4096, 128), jnp.float32)
        _a = jax.random.bernoulli(jax.random.fold_in(_gk, 2), 0.00390625, (4096, 4096))
        _a = jnp.logical_or(_a, jnp.swapaxes(_a, -1, -2))
        _a = jnp.logical_or(_a, jnp.eye(4096, dtype=bool))
        _af = _a.astype(jnp.float32)
        _af = _af * jax.random.uniform(jax.random.fold_in(_gk, 3), (4096, 4096), jnp.float32, 0.05, 5.41998)
        adj = _af
        return (x, adj)
    x, adj = _rec_inputs()

    def _L0_gnn_setup():
        import jax, jax.numpy as jnp
        import numpy as np
        N = 4096
        C = 128
        key = jax.random.key(seed)
        k1, k2, k3 = jax.random.split(key, 3)
        x = jax.random.normal(k1, (N, C), dtype=jnp.float32)
        evals = jax.random.uniform(k2, (N,), dtype=jnp.float32)
        evecs = jax.random.normal(k3, (N, N), dtype=jnp.float32)
        t = jnp.ones((1,), dtype=jnp.float32)
        return {'x': x, 'evals': evals, 'evecs': evecs, 't': t}
    _L0_gnn_all = _L0_gnn_setup()
    _L0_gnn_in = {k: v for k, v in _L0_gnn_all.items() if k in ('evals', 't')}
    del _L0_gnn_all

    def _L1_gnn_setup():
        import jax, jax.numpy as jnp
        import numpy as np
        N = 4096
        D = 128
        CUTOFF = 1.0
        MU = 1.0
        SIGMA = 0.5

        def sensitivity(r, mu, sigma):
            return jnp.exp(-(1.0 / r - 1.0 / mu) ** 2 / (2.0 * sigma * sigma))
        key = jax.random.key(seed)
        k_z, k_d, k_w = jax.random.split(key, 3)
        z = jax.random.normal(k_z, (N, D), dtype=jnp.float32)
        dist_matrix = jax.random.uniform(k_d, (N, N), dtype=jnp.float32) * 2.0 + 0.05
        W = jax.random.normal(k_w, (D, D), dtype=jnp.float32)
        B = jnp.zeros((D,), dtype=jnp.float32)
        return {'z': z, 'dist_matrix': dist_matrix, 'W': W, 'B': B}
    _L1_gnn_all = _L1_gnn_setup()
    _L1_gnn_in = {k: v for k, v in _L1_gnn_all.items() if k in ('W', 'B')}
    del _L1_gnn_all
    return {'x': x, 'adj': adj, 'L0_gnn_evals': _L0_gnn_in['evals'], 'L0_gnn_t': _L0_gnn_in['t'], 'L1_gnn_W': _L1_gnn_in['W'], 'L1_gnn_B': _L1_gnn_in['B']}

def reference(x, adj, L0_gnn_evals, L0_gnn_t, L1_gnn_W, L1_gnn_B):
    import jax
    import jax.numpy as jnp

    def _L0_gnn_ref(x, evals, evecs, t):
        import jax, jax.numpy as jnp
        import numpy as np
        N = 4096
        C = 128
        t_eff = jnp.clip(t[0], 1e-08, None)
        x_spec = jnp.einsum('nk,nc->kc', evecs, x)
        coefs = jnp.exp(-evals * t_eff)[:, None]
        out = jnp.einsum('nk,kc->nc', evecs, coefs * x_spec)
        return out

    def _L1_gnn_ref(z, dist_matrix, W, B):
        import jax, jax.numpy as jnp
        import numpy as np
        N = 4096
        D = 128
        CUTOFF = 1.0
        MU = 1.0
        SIGMA = 0.5

        def sensitivity(r, mu, sigma):
            return jnp.exp(-(1.0 / r - 1.0 / mu) ** 2 / (2.0 * sigma * sigma))
        msg = z @ W + B
        sens = sensitivity(dist_matrix, MU, SIGMA)
        weights = jnp.where(dist_matrix < CUTOFF, sens, 0.0)
        return weights @ msg
    h = jnp.maximum(_layernorm(x, axis=-1), 0.0)
    x = x + _L0_gnn_ref(h, L0_gnn_evals, adj, L0_gnn_t)
    h = jnp.maximum(_layernorm(x, axis=-1), 0.0)
    x = x + _L1_gnn_ref(h, adj, L1_gnn_W, L1_gnn_B)
    return x

_drawn_inputs = setup_inputs


def setup_inputs(seed=0):
    import zlib

    import numpy as np

    out = dict(_drawn_inputs(seed))
    spreads = {'L1_gnn_B': (0.0, 0.8)}
    factors = {'L1_gnn_W': 8.0}
    for name, (base, spread) in spreads.items():
        noise = np.random.default_rng([zlib.crc32(name.encode()), seed]).standard_normal(out[name].shape)
        drawn = base * np.exp(spread * noise) if base else spread * noise
        out[name] = jnp.asarray(drawn.astype(out[name].dtype))
    for name, factor in factors.items():
        out[name] = (out[name] * factor).astype(out[name].dtype)
    return out
```

```python
import concourse.bass as bass
from concourse import mybir
from contextlib import ExitStack


def adjacency_diffusion_message_kernel(nc: bass.Bass, x_in: bass.AP, adj: bass.AP, evals: bass.AP, t_in: bass.AP,
                                       w_in: bass.AP, b_in: bass.AP, out: bass.AP):
    fp32 = mybir.dt.float32
    ALU = mybir.AluOpType
    ACT = mybir.ActivationFunctionType

    P = 128
    N, C = x_in.shape
    BLOCKS = 4
    ROWS = BLOCKS * P
    TILES = 8
    COLS = TILES * P
    CHUNKS = N // ROWS
    STRIPS = N // COLS
    UNITS = CHUNKS * STRIPS
    BODY = 8
    BODIES = UNITS // BODY
    SPECTRUM, DIFFUSE, MESSAGE, DRAIN = range(4)
    N_W = {SPECTRUM: 2, DIFFUSE: 3, MESSAGE: 3}
    FIRST_W = {SPECTRUM: 0, DIFFUSE: 2, MESSAGE: 5}
    STORED = FIRST_W[MESSAGE]
    W_MAX = max(N_W.values())
    GROUPS = 4
    RING = 4
    LOADS = UNITS // RING
    MSG_LAG = 4
    EPS = 1e-5
    T_MIN = 1e-8
    R_TINY = float(2.0 ** -30)
    SIGN_OFF = 0x7FFFFFFF
    assert N_W[SPECTRUM] == 2 and FIRST_W[DIFFUSE] == N_W[SPECTRUM]
    assert STORED == N_W[SPECTRUM] + N_W[DIFFUSE] and STORED + N_W[MESSAGE] == TILES

    adj_full = adj.rearrange("(n b p) (k c) -> n k p b c", b=BLOCKS, p=P, c=COLS)
    x_chunks = x_in.rearrange("(n b p) c -> n p b c", b=BLOCKS, p=P)
    out_chunks = out.rearrange("(n b p) c -> n p b c", b=BLOCKS, p=P)
    w_dram = nc.dram_tensor("weights_t", [CHUNKS, STRIPS, P, STORED, ROWS], fp32).ap()

    ctx = ExitStack()
    with ctx:
        def sb(name, shape):
            return ctx.enter_context(nc.sbuf_tensor(name, shape, fp32))

        def sem(name):
            return ctx.enter_context(nc.semaphore(name))

        unit = sb("unit", [P, RING, BLOCKS * COLS])
        unit_full = unit[:, :, :].rearrange("p r (b c) -> p r b c", b=BLOCKS)
        MSG_COLS = N_W[MESSAGE] * P
        E_PART = BLOCKS * MSG_COLS
        unit_msg = unit[:, :, 0:E_PART].rearrange("p r (b c) -> p r b c", b=BLOCKS)
        w_back = unit[:, :, E_PART:E_PART + STORED * ROWS].rearrange("p r (t n) -> p r t n", t=STORED)
        x = sb("x", [P, CHUNKS, BLOCKS, C])
        h = sb("h", [P, CHUNKS, BLOCKS, C])
        msg = h
        s = sb("s", [P, N // P, C])
        adj_t = sb("adj_t", [P, 2, TILES, ROWS])
        mag = sb("mag", [P, RING, W_MAX, ROWS])
        weight = sb("weight", [P, RING, W_MAX, ROWS])
        spec_t = sb("spec_t", [P, COLS])
        acc_t = sb("acc_t", [P, ROWS])
        h2 = sb("h2", [P, BLOCKS, C])
        h2_t = sb("h2_t", [P, ROWS])
        ident = sb("ident", [P, P])
        w_sb = sb("w_sb", [C, C])
        b_sb = sb("b_sb", [P, C])
        ev_rows = sb("ev_rows", [N // P, P])
        t_sb = sb("t_sb", [P, 1])
        t_neg = sb("t_neg", [P, 1])
        coef = sb("coef", [P, N // P])
        bn = sb("bn", [P, 2, BLOCKS, 6])
        mv = sb("mv", [P, 2, BLOCKS, 2])
        ln_var = sb("ln_var", [P, 2, BLOCKS])
        rstd0 = sb("rstd0", [P, 2, BLOCKS])
        newton = sb("newton", [P, 2, BLOCKS])
        rstd = sb("rstd", [P, 2, BLOCKS])
        eps_sb = sb("eps_sb", [P, 1])
        tiny_sb = sb("tiny_sb", [P, 1])

        ps = ctx.enter_context(nc.psum_tensor("ps", [P, 8, 512], fp32))

        x_here = [sem(f"x_here{c}") for c in range(CHUNKS)]
        small_here = sem("small_here")
        ident_ready = sem("ident_ready")
        eps_ready = sem("eps_ready")
        t_ready = sem("t_ready")
        ev_transposed = sem("ev_transposed")
        coef_ready = sem("coef_ready")
        unit_here = [sem(f"unit_here{i}") for i in range(RING)]
        spectrum_used = sem("spectrum_used")
        turned = [sem(f"turned{i}") for i in range(3)]
        copied = [sem(f"copied{i}") for i in range(3)]
        mag_done = sem("mag_done")
        ln_done = sem("ln_done")
        inv_done = sem("inv_done")
        z_done = sem("z_done")
        sq_done = sem("sq_done")
        exp_done = sem("exp_done")
        weight_done = sem("weight_done")
        w_stored = [sem(f"w_stored{i}") for i in range(RING)]
        w_here = [sem(f"w_here{i}") for i in range(RING)]
        spec_copied = sem("spec_copied")
        spec_turned = sem("spec_turned")
        s_ready = sem("s_ready")
        diffuse_done = sem("diffuse_done")
        message_done = sem("message_done")
        acc_copied = sem("acc_copied")
        acc_turned = sem("acc_turned")
        x1_ready = sem("x1_ready")
        bn_done = sem("bn_done")
        mv_done = sem("mv_done")
        lnvar_done = sem("lnvar_done")
        rstd0_done = sem("rstd0_done")
        nr1_done = sem("nr1_done")
        nr2_done = sem("nr2_done")
        nr3_done = sem("nr3_done")
        rstd_done = sem("rstd_done")
        centred_done = sem("centred_done")
        h_ready = sem("h_ready")
        h2_turned = sem("h2_turned")
        h2t_ready = sem("h2t_ready")
        msg_summed = sem("msg_summed")
        msg_ready = sem("msg_ready")
        out_ready = sem("out_ready")
        out_stored = sem("out_stored")

        def bodies(eng, phase, period, periods=BODY):
            for j in range(periods):
                period(phase, 0, True, j)
            if phase != DRAIN:
                with eng.Fori(1, BODIES) as b:
                    for j in range(BODY):
                        period(phase, b, False, j)

        def count(phase, b, j):
            return phase * UNITS + BODY * b + j

        def late(phase, first, j, lag):
            return phase - 1 if first and j < lag else phase

        def tails(phase, b, first, j):
            found = [(phase, 2 * b, j - 4)] if phase != DRAIN else []
            if not first:
                found += [(phase, 2 * (b - 1), j + 4), (phase, 2 * (b - 1) + 1, j)]
            elif phase > 0:
                found += [(phase - 1, CHUNKS - 2, j + 4), (phase - 1, CHUNKS - 1, j)]
            return [f for f in found if f[0] in (DIFFUSE, MESSAGE) and f[2] >= 1]

        def ended_strip(phase, b, first):
            if phase == SPECTRUM and not first:
                return b - 1
            if phase == DIFFUSE and first:
                return STRIPS - 1
            return None

        def copied_count(phase, u):
            if phase == DIFFUSE:
                return GROUPS * u + (FIRST_W[DIFFUSE] + N_W[DIFFUSE] - 1) // 2 + 1
            return u + 1

        def w_tiles(phase):
            first_tile = FIRST_W[DIFFUSE] if phase == DIFFUSE else 0
            return slice(first_tile, first_tile + N_W[phase])

        def parity(j, step):
            return 1 if step == j else 0

        def tail_bank(phase, chunk_parity, last):
            if phase == MESSAGE:
                return chunk_parity
            return 1 if last else 2 + chunk_parity

        block = ctx.enter_context(nc.Block())

        @block.sync
        def _(sp):
            def period(phase, b, first, j):
                g = count(phase, b, j)
                u = BODY * b + j
                slot = j % RING
                if phase != DRAIN:
                    old = late(phase, first, j, RING)
                    if old == SPECTRUM:
                        sp.wait_ge(spectrum_used, g - RING + 1)
                    elif old == DIFFUSE:
                        sp.wait_ge(turned[DIFFUSE], GROUPS * (g - RING - UNITS) + GROUPS)
                    elif old == MESSAGE:
                        sp.wait_ge(turned[MESSAGE], u - RING + 1)
                    if phase == SPECTRUM:
                        src, dst = adj_full[j, b], unit_full[:, slot]
                    elif phase == DIFFUSE:
                        src, dst = adj_full[2 * b + j // STRIPS, j % STRIPS], unit_full[:, slot]
                    else:
                        src = adj_full[2 * b + j // STRIPS, j % STRIPS][:, :, STORED * P:COLS]
                        dst = unit_msg[:, slot]
                    sp.dma_start(dst, src).then_inc(unit_here[slot], 16)
                ph = late(phase, first, j, 7)
                if ph in (SPECTRUM, DIFFUSE):
                    jj = (j - 7) % BODY
                    bb = b if j >= 7 else (BODIES - 1 if first else b - 1)
                    chunk, strip = (jj, bb) if ph == SPECTRUM else (2 * bb + jj // STRIPS, jj % STRIPS)
                    f = FIRST_W[ph]
                    sp.wait_ge(weight_done, count(ph, bb, jj) + 1)
                    sp.dma_start(w_dram[chunk, strip][:, f:f + N_W[ph], :],
                                 weight[:, jj % RING, 0:N_W[ph], :]).then_inc(w_stored[jj % RING], 16)
                if late(phase, first, j, 4) == MESSAGE:
                    jj = (j - 4) % BODY
                    bb = b if j >= 4 else (BODIES - 1 if first else b - 1)
                    v = BODY * bb + jj
                    sp.wait_ge(x_here[0], 16)
                    sp.wait_ge(w_stored[jj % RING], 16 * (LOADS + BODY // RING * bb + jj // RING + 1))
                    if phase == MESSAGE and first and j == 4:
                        for i in range(RING):
                            sp.wait_ge(w_stored[i], 16 * LOADS)
                    if late(phase, first, j, 4 + RING) == MESSAGE:
                        sp.wait_ge(message_done, v - RING + 1)
                    sp.dma_start(w_back[:, jj % RING],
                                 w_dram[2 * bb + jj // STRIPS, jj % STRIPS]).then_inc(w_here[jj % RING], 16)

            sp.dma_start(x[:, 0], x_chunks[0]).then_inc(x_here[0], 16)
            sp.dma_start(unit_full[:, 0], adj_full[0, 0]).then_inc(unit_here[0], 16)
            sp.dma_start(x[:, 1], x_chunks[1]).then_inc(x_here[1], 16)
            for j in range(1, BODY):
                period(SPECTRUM, 0, True, j)
                if j + 1 < CHUNKS:
                    sp.dma_start(x[:, j + 1], x_chunks[j + 1]).then_inc(x_here[j + 1], 16)
            with sp.Fori(1, BODIES) as b:
                for j in range(BODY):
                    period(SPECTRUM, b, False, j)
            bodies(sp, DIFFUSE, period)
            bodies(sp, MESSAGE, period)
            bodies(sp, DRAIN, period, 4)

        @block.gpsimd
        def _(pool):
            pool.dma_start(ev_rows[:, :], evals.rearrange("(t p) -> t p", p=P)).then_inc(small_here, 16)
            pool.dma_start(t_sb[:, :], t_in.partition_broadcast(P)).then_inc(small_here, 16)
            pool.dma_start(w_sb[:, :], w_in).then_inc(small_here, 16)
            pool.dma_start(b_sb[:, :], b_in.partition_broadcast(P)).then_inc(small_here, 16)
            nc.gpsimd.memset(tiny_sb[:, :], R_TINY).then_inc(eps_ready, 1)
            nc.gpsimd.memset(eps_sb[:, :], EPS).then_inc(eps_ready, 1)
            nc.gpsimd.memset(ident[:, :], 0.0).then_inc(ident_ready, 1)
            pool.wait_ge(ident_ready, 1)
            nc.gpsimd.affine_select(out=ident[:, :], in_=ident[:, :], compare_op=ALU.not_equal, fill=1.0, base=0,
                                    pattern=[[-1, P]], channel_multiplier=1).then_inc(ident_ready, 1)

        @block.scalar
        def _(act):
            def copy_unit(phase, b, first, j, q):
                g = count(phase, b, j)
                u = BODY * b + j
                if not (phase == SPECTRUM and first and j < 2):
                    act.wait_ge(z_done, g - 1)
                if phase == DIFFUSE:
                    if not (first and j < 2):
                        act.wait_ge(diffuse_done, GROUPS * (u - 2) + q + 1)
                    act.wait_ge(turned[DIFFUSE], GROUPS * u + q + 1)
                    bank, tile, n = 4 + 2 * (q % 2), 2 * q, 2
                elif phase == SPECTRUM:
                    act.wait_ge(turned[SPECTRUM], u + 1)
                    bank, tile, n = 4 + 2 * (j % 2), 0, N_W[SPECTRUM]
                else:
                    if first and j < 2:
                        act.wait_ge(diffuse_done, GROUPS * (UNITS - 2 + j) + GROUPS)
                    act.wait_ge(turned[MESSAGE], u + 1)
                    bank, tile, n = (2 if j % 2 else 5), 0, N_W[MESSAGE]
                nc.scalar.activation(adj_t[:, j % 2, tile:tile + n, :], ps[:, bank:bank + n, :],
                                     ACT.Copy).then_inc(copied[phase], 1)

            def ln_unit(phase, b, first, j):
                ph = late(phase, first, j, 1)
                if ph not in (SPECTRUM, DIFFUSE, MESSAGE):
                    return
                g = count(phase, b, j) - 1
                slot, n = (j - 1) % RING, N_W[ph]
                act.wait_ge(mag_done, g + 1)
                old = late(phase, first, j, 1 + RING)
                if old in (SPECTRUM, DIFFUSE):
                    bb = b if j >= 1 + RING else (b - 1 if not first else BODIES - 1)
                    act.wait_ge(w_stored[slot],
                                16 * (LOADS * old + BODY // RING * bb + ((j - 1 - RING) % BODY) // RING + 1))
                elif old == MESSAGE:
                    act.wait_ge(message_done, g - RING - MESSAGE * UNITS + 1)
                nc.scalar.activation(weight[:, slot, 0:n, :], mag[:, slot, 0:n, :], ACT.Ln,
                                     bias=tiny_sb[:, :]).then_inc(ln_done, 1)

            def square_unit(phase, b, first, j):
                ph = late(phase, first, j, 2)
                if ph not in (SPECTRUM, DIFFUSE, MESSAGE):
                    return
                g = count(phase, b, j) - 2
                slot, n = (j - 2) % RING, N_W[ph]
                act.wait_ge(z_done, g + 1)
                nc.scalar.activation(weight[:, slot, 0:n, :], mag[:, slot, 0:n, :],
                                     ACT.Square).then_inc(sq_done, 1)

            def inv_unit(phase, b, first, j):
                ph = late(phase, first, j, 1)
                if ph not in (SPECTRUM, DIFFUSE, MESSAGE):
                    return
                g = count(phase, b, j) - 1
                slot, n = (j - 1) % RING, N_W[ph]
                act.wait_ge(ln_done, g + 1)
                nc.scalar.activation(weight[:, slot, 0:n, :], weight[:, slot, 0:n, :], ACT.Exp,
                                     scale=-1.0).then_inc(inv_done, 1)

            def exp_unit(phase, b, first, j):
                ph = late(phase, first, j, 2)
                if ph not in (SPECTRUM, DIFFUSE, MESSAGE):
                    return
                g = count(phase, b, j) - 2
                slot, n = (j - 2) % RING, N_W[ph]
                act.wait_ge(sq_done, g + 1)
                nc.scalar.activation(weight[:, slot, 0:n, :], weight[:, slot, 0:n, :], ACT.Exp,
                                     scale=-2.0).then_inc(exp_done, 1)

            def rstd_start(n, par):
                act.wait_ge(mv_done, n + 1)
                if not isinstance(n, int) or n >= 2:
                    act.wait_ge(rstd_done, n - 1)
                nc.scalar.activation(ln_var[:, par], mv[:, par, :, 1], ACT.Ln,
                                     bias=eps_sb[:, :]).then_inc(lnvar_done, 1)
                act.wait_ge(lnvar_done, n + 1)
                nc.scalar.activation(rstd0[:, par], ln_var[:, par], ACT.Exp, scale=-0.5).then_inc(rstd0_done, 1)

            def period(phase, b, first, j):
                strip = ended_strip(phase, b, first)
                if strip is not None and j == 0:
                    act.wait_ge(spectrum_used, BODY * (strip + 1))
                    nc.scalar.activation(spec_t[:, :], ps[:, 0:2, :], ACT.Copy).then_inc(spec_copied, 1)
                for ph, chunk, step in tails(phase, b, first, j):
                    n = chunk + (CHUNKS if ph == MESSAGE else 0)
                    if (ph, step) in ((DIFFUSE, 1), (MESSAGE, 4)):
                        par = parity(j, step)
                        if ph == DIFFUSE:
                            act.wait_ge(diffuse_done, GROUPS * STRIPS * (chunk + 1))
                        else:
                            act.wait_ge(message_done, STRIPS * (chunk + 1))
                        act.wait_ge(acc_turned, n)
                        nc.scalar.activation(acc_t[:, :], ps[:, par, :], ACT.Copy).then_inc(acc_copied, 1)
                    if (ph, step) == (DIFFUSE, 4):
                        bank = tail_bank(DIFFUSE, parity(j, step), ph != phase and parity(j, step) == 1)
                        act.wait_ge(h2_turned, chunk + 1)
                        nc.scalar.activation(h2_t[:, :], ps[:, bank, :], ACT.Relu).then_inc(h2t_ready, 1)
                    if (ph, step) == (MESSAGE, 6):
                        act.wait_ge(out_ready, chunk + 1)
                        act.dma_start(out_chunks[chunk], x[:, chunk]).then_inc(out_stored, 16)
                if phase == DIFFUSE:
                    copy_unit(phase, b, first, j, 0)
                    ln_unit(phase, b, first, j)
                    copy_unit(phase, b, first, j, 1)
                    square_unit(phase, b, first, j)
                    copy_unit(phase, b, first, j, 2)
                    inv_unit(phase, b, first, j)
                    copy_unit(phase, b, first, j, 3)
                    exp_unit(phase, b, first, j)
                else:
                    if phase != DRAIN:
                        copy_unit(phase, b, first, j, 0)
                    ln_unit(phase, b, first, j)
                    square_unit(phase, b, first, j)
                    inv_unit(phase, b, first, j)
                    exp_unit(phase, b, first, j)
                for ph, chunk, step in tails(phase, b, first, j):
                    if (ph, step) == (DIFFUSE, 2):
                        rstd_start(CHUNKS + chunk, parity(j, step))
                if phase == SPECTRUM and first and j + 2 < CHUNKS:
                    rstd_start(j + 2, j % 2)

            nc.scalar.preload_act_table_set("natural_log_exp_and_others")
            act.wait_ge(eps_ready, 2)
            rstd_start(0, 0)
            act.wait_ge(ev_transposed, 1)
            act.wait_ge(t_ready, 1)
            nc.scalar.activation(coef[:, :], ps[:, 2, 0:N // P], ACT.Exp, scale=t_neg[:, :]).then_inc(coef_ready, 1)
            rstd_start(1, 1)
            bodies(act, SPECTRUM, period)
            bodies(act, DIFFUSE, period)
            bodies(act, MESSAGE, period)
            bodies(act, DRAIN, period, 7)
            act.wait_ge(out_stored, 16 * CHUNKS)

        @block.vector
        def _(dve):
            def mag_unit(phase, b, first, j):
                if phase == DRAIN:
                    return
                u, n = BODY * b + j, N_W[phase]
                dve.wait_ge(copied[phase], copied_count(phase, u))
                nc.vector.tensor_scalar(mag[:, j % RING, 0:n, :].bitcast(mybir.dt.int32),
                                        adj_t[:, j % 2, w_tiles(phase), :].bitcast(mybir.dt.int32),
                                        SIGN_OFF, None, ALU.bitwise_and).then_inc(mag_done, 1)

            def z_unit(phase, b, first, j):
                ph = late(phase, first, j, 1)
                if ph not in (SPECTRUM, DIFFUSE, MESSAGE):
                    return
                g, slot, n = count(phase, b, j) - 1, (j - 1) % RING, N_W[ph]
                dve.wait_ge(inv_done, g + 1)
                nc.vector.scalar_tensor_tensor(out=mag[:, slot, 0:n, :], in0=adj_t[:, (j - 1) % 2, w_tiles(ph), :],
                                               scalar=1.0, in1=weight[:, slot, 0:n, :], op0=ALU.subtract,
                                               op1=ALU.mult).then_inc(z_done, 1)

            def mask_unit(phase, b, first, j):
                ph = late(phase, first, j, 3)
                if ph not in (SPECTRUM, DIFFUSE, MESSAGE):
                    return
                g, slot, n = count(phase, b, j) - 3, (j - 3) % RING, N_W[ph]
                dve.wait_ge(exp_done, g + 1)
                nc.vector.scalar_tensor_tensor(out=weight[:, slot, 0:n, :], in0=mag[:, slot, 0:n, :], scalar=0.0,
                                               in1=weight[:, slot, 0:n, :], op0=ALU.is_lt,
                                               op1=ALU.mult).then_inc(weight_done, 1)

            def ln_stats(n, par, rows):
                nc.vector.memset(newton[:, par, 1:2], 0.0)
                for i in range(BLOCKS):
                    last = nc.vector.bn_stats(bn[:, par, i], rows[:, i])
                last.then_inc(bn_done, 1)
                dve.wait_ge(bn_done, n + 1)
                nc.vector.memset(newton[:, par, 0:1], 0.0)
                for i in range(BLOCKS):
                    last = nc.vector.bn_aggr(mv[:, par, i], bn[:, par, i])
                last.then_inc(mv_done, 1)

            def ln_apply(n, par, rows, centred):
                dve.wait_ge(rstd0_done, n + 1)
                nc.vector.tensor_tensor(newton[:, par], rstd0[:, par], rstd0[:, par], ALU.mult).then_inc(nr1_done, 1)
                dve.wait_ge(nr1_done, n + 1)
                nc.vector.scalar_tensor_tensor(out=newton[:, par], in0=mv[:, par, :, 1], scalar=EPS,
                                               in1=newton[:, par], op0=ALU.add, op1=ALU.mult).then_inc(nr2_done, 1)
                dve.wait_ge(nr2_done, n + 1)
                nc.vector.tensor_scalar(newton[:, par], newton[:, par], -0.5, 1.5, ALU.mult, ALU.add)\
                    .then_inc(nr3_done, 1)
                dve.wait_ge(nr3_done, n + 1)
                nc.vector.tensor_tensor(rstd[:, par], newton[:, par], rstd0[:, par], ALU.mult).then_inc(rstd_done, 1)
                dve.wait_ge(rstd_done, n + 1)
                for i in range(BLOCKS):
                    last = nc.vector.tensor_scalar(centred[:, i], rows[:, i], mv[:, par, i, 0:1],
                                                   rstd[:, par, i:i + 1], ALU.subtract, ALU.mult)
                last.then_inc(centred_done, 1)

            def ln_x_stats(c):
                dve.wait_ge(x_here[c], 16)
                ln_stats(c, c % 2, x[:, c])

            def ln_x_apply(c):
                ln_apply(c, c % 2, x[:, c], h[:, c])
                dve.wait_ge(centred_done, c + 1)
                nc.vector.tensor_scalar(h[:, c], h[:, c], 0.0, None, ALU.max).then_inc(h_ready, 1)

            def period(phase, b, first, j):
                strip = ended_strip(phase, b, first)
                if strip is not None and j == 2:
                    dve.wait_ge(spec_turned, strip + 1)
                    dve.wait_ge(coef_ready, 1)
                    nc.vector.tensor_tensor(
                        s[:, bass.ds(strip * TILES, TILES), :],
                        ps[:, 2:4, :].rearrange("p a (t c) -> p (a t) c", c=C),
                        coef[:, bass.ds(strip * TILES, TILES)].unsqueeze(2).broadcast_to([P, TILES, C]),
                        ALU.mult).then_inc(s_ready, 1)
                for ph, chunk, step in tails(phase, b, first, j):
                    par = parity(j, step)
                    bank = ps[:, tail_bank(ph, par, ph != phase and par == 1), :]\
                        .rearrange("p (b c) -> p b c", c=C)
                    if (ph, step) == (DIFFUSE, 2):
                        dve.wait_ge(acc_turned, chunk + 1)
                        nc.vector.tensor_tensor(x[:, chunk], x[:, chunk], bank, ALU.add).then_inc(x1_ready, 1)
                        dve.wait_ge(x1_ready, chunk + 1)
                        ln_stats(CHUNKS + chunk, par, x[:, chunk])
                    if (ph, step) == (DIFFUSE, 3):
                        dve.wait_ge(h2_turned, chunk)
                        ln_apply(CHUNKS + chunk, par, x[:, chunk], h2)
                    if (ph, step) == (DIFFUSE, 5):
                        dve.wait_ge(msg_summed, chunk + 1)
                        nc.vector.tensor_tensor(msg[:, chunk], bank, b_sb[:, :].unsqueeze(1).broadcast_to([P, BLOCKS, C]),
                                                ALU.add).then_inc(msg_ready, 1)
                    if (ph, step) == (MESSAGE, 5):
                        dve.wait_ge(acc_turned, CHUNKS + chunk + 1)
                        nc.vector.tensor_tensor(x[:, chunk], x[:, chunk], bank, ALU.add).then_inc(out_ready, 1)
                mag_unit(phase, b, first, j)
                mask_unit(phase, b, first, j)
                if phase == SPECTRUM and first and j + 1 < CHUNKS:
                    ln_x_apply(j + 1)
                z_unit(phase, b, first, j)
                if phase == SPECTRUM and first and j + 2 < CHUNKS:
                    ln_x_stats(j + 2)

            ln_x_stats(0)
            ln_x_stats(1)
            ln_x_apply(0)
            dve.wait_ge(small_here, 64)
            nc.vector.tensor_scalar(t_neg[:, :], t_sb[:, :], T_MIN, -1.0, ALU.max, ALU.mult).then_inc(t_ready, 1)
            bodies(dve, SPECTRUM, period)
            bodies(dve, DIFFUSE, period)
            bodies(dve, MESSAGE, period)
            bodies(dve, DRAIN, period, 7)

        @block.tensor
        def _(pe):
            def unit_arrived(phase, b, j):
                pe.wait_ge(unit_here[j % RING], 16 * (LOADS * phase + BODY // RING * b + j // RING + 1))

            def turn_unit(phase, b, first, j):
                u = BODY * b + j
                bank = 4 + 2 * (j % 2) if phase == SPECTRUM else (2 if j % 2 else 5)
                src = unit_full if phase == SPECTRUM else unit_msg
                if not (first and j < 2):
                    pe.wait_ge(copied[phase], u - 1)
                elif phase == MESSAGE:
                    pe.wait_ge(copied[DIFFUSE], GROUPS * UNITS)
                    if j == 1:
                        pe.wait_ge(msg_ready, CHUNKS - 1)
                for t in range(N_W[phase]):
                    for i in range(BLOCKS):
                        last = nc.tensor.transpose(ps[:, bank + t, i * P:(i + 1) * P],
                                                   src[:, j % RING, i, t * P:(t + 1) * P], ident[:, :])
                last.then_inc(turned[phase], 1)

            def spectrum_period(phase, b, first, j):
                unit_arrived(phase, b, j)
                turn_unit(phase, b, first, j)
                if first:
                    pe.wait_ge(h_ready, j + 1)
                elif j == 0:
                    pe.wait_ge(spec_copied, b)
                for i in range(BLOCKS):
                    for half in range(2):
                        last = nc.tensor.matmul(ps[:, half, :], h[:, j, i, :],
                                                unit_full[:, j % RING, i, half * 512:(half + 1) * 512],
                                                start=(j == 0 and i == 0), stop=(j == BODY - 1 and i == BLOCKS - 1))
                last.then_inc(spectrum_used, 1)
                strip_tail(phase, b, first, j)

            def strip_tail(phase, b, first, j):
                strip = ended_strip(phase, b, first)
                if strip is None or j != 1:
                    return
                pe.wait_ge(spec_copied, strip + 1)
                pe.wait_ge(coef_ready, 1)
                for t in range(TILES):
                    last = nc.tensor.transpose(ps[:, 2 + t // 4, (t % 4) * P:(t % 4 + 1) * P],
                                               spec_t[:, t * P:(t + 1) * P], ident[:, :])
                last.then_inc(spec_turned, 1)

            def diffuse_turn(b, first, j, q):
                u = BODY * b + j
                n = GROUPS * u + q
                if first and j == 0 and q < 2:
                    pe.wait_ge(copied[SPECTRUM], UNITS)
                else:
                    pe.wait_ge(copied[DIFFUSE], n - 1)
                for t in range(2):
                    for i in range(BLOCKS):
                        c = (2 * q + t) * P
                        last = nc.tensor.transpose(ps[:, 4 + 2 * (q % 2) + t, i * P:(i + 1) * P],
                                                   unit_full[:, j % RING, i, c:c + P], ident[:, :])
                last.then_inc(turned[DIFFUSE], 1)

            def diffuse_sum(b, first, j, q):
                u = BODY * b + j
                strip = j % STRIPS
                acc = j // STRIPS
                pe.wait_ge(copied[DIFFUSE], GROUPS * u + q + 1)
                if q == 0 and first and j < STRIPS:
                    pe.wait_ge(s_ready, strip + 1)
                if q == 0 and strip == 0 and not first:
                    pe.wait_ge(acc_copied, 2 * b + acc - 1)
                for t in range(2):
                    tile = 2 * q + t
                    last = nc.tensor.matmul(ps[:, acc, :], s[:, strip * TILES + tile, :], adj_t[:, j % 2, tile, :],
                                            start=(strip == 0 and tile == 0),
                                            stop=(strip == STRIPS - 1 and tile == TILES - 1))
                last.then_inc(diffuse_done, 1)

            def diffuse_sum_late(phase, b, first, j, q):
                if q >= 2:
                    diffuse_sum(b, first, j, q - 2)
                elif j > 0:
                    diffuse_sum(b, first, j - 1, q + 2)
                elif not first:
                    diffuse_sum(b - 1, False, BODY - 1, q + 2)

            def turn_acc(ph, chunk, bank):
                n = chunk + (CHUNKS if ph == MESSAGE else 0)
                pe.wait_ge(acc_copied, n + 1)
                for i in range(BLOCKS):
                    last = nc.tensor.transpose(ps[:, bank, i * P:(i + 1) * P], acc_t[:, i * P:(i + 1) * P],
                                               ident[:, :])
                last.then_inc(acc_turned, 1)

            def chunk_tails(phase, b, first, j):
                for ph, chunk, step in tails(phase, b, first, j):
                    par = parity(j, step)
                    bank = tail_bank(ph, par, ph != phase and par == 1)
                    if (ph, step) == (DIFFUSE, 1):
                        if first and ph == phase:
                            pe.wait_ge(s_ready, STRIPS)
                        turn_acc(ph, chunk, bank)
                    if (ph, step) == (DIFFUSE, 3):
                        pe.wait_ge(centred_done, CHUNKS + chunk + 1)
                        for i in range(BLOCKS):
                            last = nc.tensor.transpose(ps[:, bank, i * P:(i + 1) * P], h2[:, i], ident[:, :])
                        last.then_inc(h2_turned, 1)
                    if (ph, step) == (DIFFUSE, 4):
                        pe.wait_ge(h2t_ready, chunk + 1)
                        for i in range(BLOCKS):
                            last = nc.tensor.matmul(ps[:, bank, i * P:(i + 1) * P], h2_t[:, i * P:(i + 1) * P],
                                                    w_sb[:, :], start=True, stop=True)
                        last.then_inc(msg_summed, 1)
                    if (ph, step) == (MESSAGE, 4):
                        turn_acc(ph, chunk, bank)

            def diffuse_period(phase, b, first, j):
                unit_arrived(phase, b, j)
                for q in range(GROUPS):
                    diffuse_turn(b, first, j, q)
                    if first and j == 0 and q == 2:
                        pe.wait_ge(spec_copied, STRIPS)
                    diffuse_sum_late(phase, b, first, j, q)
                    if q == 1:
                        strip_tail(phase, b, first, j)
                        chunk_tails(phase, b, first, j)

            def message_sum(phase, b, first, j):
                ph = late(phase, first, j, MSG_LAG)
                if ph != MESSAGE:
                    return
                g = count(phase, b, j) - MSG_LAG
                jj = (j - MSG_LAG) % BODY
                bb = b if j >= MSG_LAG else (BODIES - 1 if first else b - 1)
                strip, acc, slot = jj % STRIPS, jj // STRIPS, jj % RING
                if strip == 0:
                    if first and phase == MESSAGE:
                        pe.wait_ge(acc_copied, CHUNKS - 1)
                    else:
                        pe.wait_ge(msg_ready, CHUNKS)
                if first and phase == MESSAGE:
                    pe.wait_ge(msg_ready, 2 * strip + 2)
                pe.wait_ge(w_here[slot], 16 * (BODY // RING * bb + jj // RING + 1))
                for t in range(STORED):
                    nc.tensor.matmul(ps[:, acc, :], msg[:, 2 * strip + t // 4, t % 4, :], w_back[:, slot, t, :],
                                     start=(strip == 0 and t == 0), stop=False)
                pe.wait_ge(weight_done, g + 1)
                for t in range(STORED, TILES):
                    last = nc.tensor.matmul(ps[:, acc, :], msg[:, 2 * strip + t // 4, t % 4, :],
                                            weight[:, slot, t - STORED, :],
                                            start=False, stop=(strip == STRIPS - 1 and t == TILES - 1))
                last.then_inc(message_done, 1)

            def message_period(phase, b, first, j):
                if first and j == 0:
                    diffuse_sum(BODIES - 1, False, BODY - 1, 2)
                    diffuse_sum(BODIES - 1, False, BODY - 1, 3)
                unit_arrived(phase, b, j)
                turn_unit(phase, b, first, j)
                message_sum(phase, b, first, j)
                chunk_tails(phase, b, first, j)

            def drain_period(phase, b, first, j):
                message_sum(phase, b, first, j)
                chunk_tails(phase, b, first, j)

            pe.wait_ge(ident_ready, 2)
            pe.wait_ge(small_here, 64)
            nc.tensor.transpose(ps[:, 2, 0:N // P], ev_rows[:, :], ident[0:N // P, 0:N // P])\
                .then_inc(ev_transposed, 1)
            bodies(pe, SPECTRUM, spectrum_period)
            bodies(pe, DIFFUSE, diffuse_period)
            bodies(pe, MESSAGE, message_period)
            bodies(pe, DRAIN, drain_period, 7)


_INS = ["x", "adj", "L0_gnn_evals", "L0_gnn_t", "L1_gnn_W", "L1_gnn_B"]


def kernel(**inputs):
    import numpy as _np
    import concourse.bacc as _bacc
    from concourse import mybir as _mybir
    from concourse.bass_utils import run_bass_kernel_spmd as _run

    nc = _bacc.Bacc("TRN2", target_bir_lowering=False, num_devices=1)
    arrays, args = {}, []
    for name in _INS:
        a = _np.ascontiguousarray(inputs[name])
        arrays[f"in_{name}_dram"] = a
        args.append(nc.dram_tensor(f"in_{name}_dram", a.shape, _mybir.dt.from_np(a.dtype), kind="ExternalInput").ap())
    rows, cols = arrays["in_x_dram"].shape
    out = nc.dram_tensor("out_dram", (rows, cols), _mybir.dt.float32, kind="ExternalOutput").ap()
    adjacency_diffusion_message_kernel(nc, *args, out)
    r = _run(nc, [arrays], core_ids=[0])
    return r.results[0]["out_dram"]
```

```python
import concourse.bass as bass
from concourse import mybir
from contextlib import ExitStack


def adjacency_diffusion_message_kernel(nc: bass.Bass, x_in: bass.AP, adj: bass.AP, evals: bass.AP, t_in: bass.AP,
                                       w_in: bass.AP, b_in: bass.AP, out: bass.AP):
    fp32 = mybir.dt.float32
    ALU = mybir.AluOpType
    ACT = mybir.ActivationFunctionType

    P = 128
    N, C = x_in.shape
    BLOCKS = 4
    ROWS = BLOCKS * P
    TILES = 8
    COLS = TILES * P
    CHUNKS = N // ROWS
    STRIPS = N // COLS
    UNITS = CHUNKS * STRIPS
    BODY = 8
    BODIES = UNITS // BODY
    SPECTRUM, DIFFUSE, MESSAGE, DRAIN = range(4)
    N_W = {SPECTRUM: 2, DIFFUSE: 2, MESSAGE: 4}
    FIRST_W = {SPECTRUM: 0, DIFFUSE: 2, MESSAGE: 4}
    STORED = FIRST_W[MESSAGE]
    GROUPS = TILES // 2
    QUADS = 4
    B32 = 32
    R_BLOCKS = ROWS // B32
    RING = 4
    LOADS = UNITS // RING
    MSG_LAG = 4
    EPS = 1e-5
    T_MIN = 1e-8
    R_TINY = float(2.0 ** -30)
    SIGN_OFF = 0x7FFFFFFF
    assert N_W[SPECTRUM] == N_W[DIFFUSE] == FIRST_W[DIFFUSE] == 2 and TILES * B32 * QUADS == COLS
    assert STORED == N_W[SPECTRUM] + N_W[DIFFUSE] and STORED + N_W[MESSAGE] == TILES

    adj_full = adj.rearrange("(n b p) (k c) -> n k p b c", b=BLOCKS, p=P, c=COLS)
    adj_quads = adj.rearrange("(n r i) (k q c) -> n k q i r c", r=R_BLOCKS, i=B32, q=QUADS, c=COLS // QUADS)
    ev_quads = evals.rearrange("(k q t j) -> k t q j", q=QUADS, t=TILES, j=B32)
    x_chunks = x_in.rearrange("(n b p) c -> n p b c", b=BLOCKS, p=P)
    out_chunks = out.rearrange("(n b p) c -> n p b c", b=BLOCKS, p=P)
    w_dram = nc.dram_tensor("weights_t", [CHUNKS, STRIPS, P, STORED, ROWS], fp32).ap()

    ctx = ExitStack()
    with ctx:
        def sb(name, shape):
            return ctx.enter_context(nc.sbuf_tensor(name, shape, fp32))

        def sem(name):
            return ctx.enter_context(nc.semaphore(name))

        unit = sb("unit", [P, RING, BLOCKS * COLS])
        unit_full = unit[:, :, :].rearrange("p r (b c) -> p r b c", b=BLOCKS)
        unit_quads = unit[:, :, :].rearrange("p r (b c) -> p r b c", b=R_BLOCKS)
        MSG_COLS = N_W[MESSAGE] * B32
        E_PART = R_BLOCKS * MSG_COLS
        unit_msg = unit[:, :, 0:E_PART].rearrange("p r (b c) -> p r b c", b=R_BLOCKS)
        w_back = unit[:, :, E_PART:E_PART + STORED * ROWS].rearrange("p r (t n) -> p r t n", t=STORED)
        x = sb("x", [P, CHUNKS, BLOCKS, C])
        h = sb("h", [P, CHUNKS, BLOCKS, C])
        msg = h[:, :, :, :].rearrange("p n b c -> p (n b) c")
        adj_t = sb("adj_t", [P, 2, TILES, ROWS])
        work = sb("work", [P, 4, RING * 2 * ROWS])
        s = work[:, 0, :].rearrange("p (t c) -> p t c", c=C)

        def ring(first, n_quarters):
            return work[:, first:first + n_quarters, :].rearrange("p a (r n) -> p (a r) n", n=ROWS * N_W[MESSAGE]
                                                                  if n_quarters == 2 else 2 * ROWS)

        stage = ring(2, 1)
        mag = {SPECTRUM: ring(1, 1), DIFFUSE: ring(1, 1), MESSAGE: ring(0, 2)}
        weight = {SPECTRUM: ring(3, 1), DIFFUSE: ring(3, 1), MESSAGE: ring(2, 2)}
        spec_t = sb("spec_t", [P, TILES, P])
        acc_t = sb("acc_t", [P, ROWS])
        h2 = sb("h2", [P, BLOCKS, C])
        h2_t = sb("h2_t", [P, TILES, P])
        ident = sb("ident", [P, P])
        w_sb = sb("w_sb", [C, C])
        b_sb = sb("b_sb", [P, C])
        ev_rows = sb("ev_rows", [N // P, P])
        t_sb = sb("t_sb", [P, 1])
        t_neg = sb("t_neg", [P, 1])
        coef = sb("coef", [P, N // P])
        bn = sb("bn", [P, 2, BLOCKS, 6])
        mv = sb("mv", [P, 2, BLOCKS, 2])
        ln_var = sb("ln_var", [P, 2, BLOCKS])
        rstd0 = sb("rstd0", [P, 2, BLOCKS])
        newton = sb("newton", [P, 2, BLOCKS])
        rstd = sb("rstd", [P, 2, BLOCKS])
        eps_sb = sb("eps_sb", [P, 1])
        tiny_sb = sb("tiny_sb", [P, 1])

        ps = ctx.enter_context(nc.psum_tensor("ps", [P, 8, 512], fp32))

        x_here = [sem(f"x_here{c}") for c in range(CHUNKS)]
        small_here = sem("small_here")
        ident_ready = sem("ident_ready")
        eps_ready = sem("eps_ready")
        t_ready = sem("t_ready")
        ev_transposed = sem("ev_transposed")
        coef_ready = sem("coef_ready")
        unit_here = [sem(f"unit_here{i}") for i in range(RING)]
        spectrum_used = sem("spectrum_used")
        turned = sem("turned")
        copied = sem("copied")
        diffuse_turned = sem("diffuse_turned")
        message_turned = sem("message_turned")
        mag_done = sem("mag_done")
        abs_done = sem("abs_done")
        ln_done = sem("ln_done")
        inv_done = sem("inv_done")
        z_done = sem("z_done")
        sq_done = sem("sq_done")
        exp_done = sem("exp_done")
        weight_done = sem("weight_done")
        w_stored = [sem(f"w_stored{i}") for i in range(RING)]
        w_here = [sem(f"w_here{i}") for i in range(RING)]
        spec_copied = sem("spec_copied")
        spec_turned = sem("spec_turned")
        s_ready = sem("s_ready")
        diffuse_done = sem("diffuse_done")
        message_done = sem("message_done")
        acc_copied = sem("acc_copied")
        acc_turned = sem("acc_turned")
        x1_ready = sem("x1_ready")
        bn_done = sem("bn_done")
        mv_done = sem("mv_done")
        lnvar_done = sem("lnvar_done")
        rstd0_done = sem("rstd0_done")
        nr1_done = sem("nr1_done")
        nr2_done = sem("nr2_done")
        nr3_done = sem("nr3_done")
        rstd_done = sem("rstd_done")
        centred_done = sem("centred_done")
        h_ready = sem("h_ready")
        h2_turned = sem("h2_turned")
        h2t_ready = sem("h2t_ready")
        msg_summed = sem("msg_summed")
        msg_ready = sem("msg_ready")
        out_ready = sem("out_ready")
        out_stored = sem("out_stored")

        def bodies(eng, phase, period, periods=BODY):
            for j in range(periods):
                period(phase, 0, True, j)
            if phase != DRAIN:
                with eng.Fori(1, BODIES) as b:
                    for j in range(BODY):
                        period(phase, b, False, j)

        def count(phase, b, j):
            return phase * UNITS + BODY * b + j

        def late(phase, first, j, lag):
            return phase - 1 if first and j < lag else phase

        def tails(phase, b, first, j):
            found = [(phase, 2 * b, j - 4)] if phase != DRAIN else []
            if not first:
                found += [(phase, 2 * (b - 1), j + 4), (phase, 2 * (b - 1) + 1, j)]
            elif phase > 0:
                found += [(phase - 1, CHUNKS - 2, j + 4), (phase - 1, CHUNKS - 1, j)]
            return [f for f in found if f[0] in (DIFFUSE, MESSAGE) and f[2] >= 1]

        def ended_strip(phase, b, first):
            if phase == SPECTRUM and not first:
                return b - 1
            if phase == DIFFUSE and first:
                return STRIPS - 1
            return None

        def w_tiles(phase):
            first_tile = FIRST_W[DIFFUSE] if phase == DIFFUSE else 0
            return slice(first_tile, first_tile + N_W[phase])

        def from_adj(ph):
            return adj_t[:, :, w_tiles(ph), :].rearrange("p s t n -> p s (t n)")

        unit_tiles = unit[:, :, :].rearrange("p r (bq t j) -> p r t bq j", t=TILES, j=B32)

        def strip_of(phase, b, first, j, step):
            return b - 1 if not first else BODIES - 1

        def parity(j, step):
            return 1 if step == j else 0

        def tail_bank(phase, chunk_parity):
            return chunk_parity + (2 if phase == DIFFUSE else 0)

        block = ctx.enter_context(nc.Block())

        @block.sync
        def _(sp):
            def period(phase, b, first, j):
                g = count(phase, b, j)
                u = BODY * b + j
                slot = j % RING
                if phase != DRAIN:
                    old = late(phase, first, j, RING)
                    if old == SPECTRUM:
                        sp.wait_ge(spectrum_used, g - RING + 1)
                        sp.wait_ge(z_done, g - RING + 1)
                    elif old == DIFFUSE:
                        sp.wait_ge(diffuse_turned, GROUPS * (g - RING - UNITS) + GROUPS)
                    elif old == MESSAGE:
                        sp.wait_ge(message_turned, u - RING + 1)
                    if phase == SPECTRUM:
                        sp.dma_start(unit_full[:, slot], adj_full[j, b]).then_inc(unit_here[slot], 16)
                    else:
                        for q in range(QUADS):
                            src = adj_quads[2 * b + j // STRIPS, j % STRIPS, q]
                            dst = unit_quads if phase == DIFFUSE else unit_msg
                            if phase == MESSAGE:
                                src = src[:, :, STORED * B32:TILES * B32]
                            sp.dma_start(dst[q * B32:(q + 1) * B32, slot], src).then_inc(unit_here[slot], 16)
                if late(phase, first, j, BODY) == SPECTRUM:
                    bb = BODIES - 1 if first else b - 1
                    sp.wait_ge(copied, BODY * bb + j + 1)
                    sp.dma_start(w_dram[j, bb][:, 0:N_W[SPECTRUM], :],
                                 stage[:, j % RING].rearrange("p (t n) -> p t n", n=ROWS)).then_inc(w_stored[j % RING], 16)
                if late(phase, first, j, 7) == DIFFUSE:
                    jj = (j - 7) % BODY
                    bb = b if j >= 7 else (BODIES - 1 if first else b - 1)
                    f = FIRST_W[DIFFUSE]
                    sp.wait_ge(weight_done, count(DIFFUSE, bb, jj) + 1)
                    sp.dma_start(w_dram[2 * bb + jj // STRIPS, jj % STRIPS][:, f:f + N_W[DIFFUSE], :],
                                 weight[DIFFUSE][:, jj % RING].rearrange("p (t n) -> p t n", n=ROWS))\
                        .then_inc(w_stored[jj % RING], 16)
                if late(phase, first, j, 4) == MESSAGE:
                    jj = (j - 4) % BODY
                    bb = b if j >= 4 else (BODIES - 1 if first else b - 1)
                    v = BODY * bb + jj
                    sp.wait_ge(x_here[0], 16)
                    sp.wait_ge(w_stored[jj % RING], 16 * (LOADS + BODY // RING * bb + jj // RING + 1))
                    if phase == MESSAGE and first and j == 4:
                        for i in range(RING):
                            sp.wait_ge(w_stored[i], 16 * LOADS)
                    if late(phase, first, j, 4 + RING) == MESSAGE:
                        sp.wait_ge(message_done, v - RING + 1)
                    sp.dma_start(w_back[:, jj % RING],
                                 w_dram[2 * bb + jj // STRIPS, jj % STRIPS]).then_inc(w_here[jj % RING], 16)

            sp.dma_start(x[:, 0], x_chunks[0]).then_inc(x_here[0], 16)
            sp.dma_start(unit_full[:, 0], adj_full[0, 0]).then_inc(unit_here[0], 16)
            sp.dma_start(x[:, 1], x_chunks[1]).then_inc(x_here[1], 16)
            for j in range(1, BODY):
                period(SPECTRUM, 0, True, j)
                if j + 1 < CHUNKS:
                    sp.dma_start(x[:, j + 1], x_chunks[j + 1]).then_inc(x_here[j + 1], 16)
            with sp.Fori(1, BODIES) as b:
                for j in range(BODY):
                    period(SPECTRUM, b, False, j)
            bodies(sp, DIFFUSE, period)
            bodies(sp, MESSAGE, period)
            bodies(sp, DRAIN, period, 4)

        @block.gpsimd
        def _(pool):
            nc.gpsimd.memset(tiny_sb[:, :], R_TINY).then_inc(eps_ready, 1)
            nc.gpsimd.memset(eps_sb[:, :], EPS).then_inc(eps_ready, 1)
            nc.gpsimd.memset(ident[:, :], 0.0).then_inc(ident_ready, 1)
            pool.wait_ge(ident_ready, 1)
            nc.gpsimd.affine_select(out=ident[:, :], in_=ident[:, :], compare_op=ALU.not_equal, fill=1.0, base=0,
                                    pattern=[[-1, P]], channel_multiplier=1).then_inc(ident_ready, 1)

        @block.scalar
        def _(act):
            def copy_unit(phase, b, first, j):
                if late(phase, first, j, 4) != SPECTRUM:
                    return
                jj = (j - 4) % BODY
                bb = b if j >= 4 else (BODIES - 1 if first else b - 1)
                if not (phase == SPECTRUM and first):
                    act.wait_ge(w_stored[jj % RING], 16 * (BODY // RING * bb + jj // RING))
                act.wait_ge(turned, BODY * bb + jj + 1)
                bank, n = 4 + 2 * (jj % 2), N_W[SPECTRUM]
                nc.scalar.activation(stage[:, jj % RING], ps[:, bank:bank + n, :].rearrange("p t n -> p (t n)"),
                                     ACT.Copy).then_inc(copied, 1)

            def mag_unit(phase, b, first, j):
                u = BODY * b + j
                act.wait_ge(diffuse_turned, GROUPS * u + FIRST_W[DIFFUSE] // 2 + 1)
                act.wait_ge(weight_done, UNITS + u - RING + 1)
                nc.scalar.activation(mag[DIFFUSE][:, j % RING], from_adj(DIFFUSE)[:, j % 2],
                                     ACT.Abs).then_inc(abs_done, 1)

            def ln_unit(phase, b, first, j):
                ph = late(phase, first, j, 1)
                if ph not in (SPECTRUM, DIFFUSE, MESSAGE):
                    return
                g = count(phase, b, j) - 1
                slot = (j - 1) % RING
                if ph == SPECTRUM:
                    act.wait_ge(mag_done, g + 1)
                elif ph == DIFFUSE:
                    act.wait_ge(abs_done, g - UNITS + 1)
                else:
                    act.wait_ge(mag_done, g - UNITS + 1)
                old = late(phase, first, j, 1 + RING)
                bb = b if j >= 1 + RING else (b - 1 if not first else BODIES - 1)
                loads = BODY // RING * bb + ((j - 1 - RING) % BODY) // RING + 1
                if old == SPECTRUM:
                    act.wait_ge(turned, g - RING + 1)
                elif old == DIFFUSE and ph == DIFFUSE:
                    act.wait_ge(w_stored[slot], 16 * (LOADS + loads))
                elif old == DIFFUSE and j == 1:
                    for i in range(RING):
                        act.wait_ge(w_stored[i], 16 * LOADS)
                elif old == DIFFUSE and j in (3, 4):
                    for i in (2 * (j - 3), 2 * (j - 3) + 1):
                        act.wait_ge(w_stored[i], 16 * 2 * LOADS)
                elif old == MESSAGE:
                    act.wait_ge(message_done, g - RING - MESSAGE * UNITS + 1)
                nc.scalar.activation(weight[ph][:, slot], mag[ph][:, slot], ACT.Ln,
                                     bias=tiny_sb[:, :]).then_inc(ln_done, 1)

            def square_unit(phase, b, first, j):
                ph = late(phase, first, j, 2)
                if ph not in (SPECTRUM, DIFFUSE, MESSAGE):
                    return
                g = count(phase, b, j) - 2
                slot = (j - 2) % RING
                act.wait_ge(z_done, g + 1)
                nc.scalar.activation(weight[ph][:, slot], mag[ph][:, slot], ACT.Square).then_inc(sq_done, 1)

            def inv_unit(phase, b, first, j):
                ph = late(phase, first, j, 1)
                if ph not in (SPECTRUM, DIFFUSE, MESSAGE):
                    return
                g = count(phase, b, j) - 1
                slot = (j - 1) % RING
                act.wait_ge(ln_done, g + 1)
                nc.scalar.activation(weight[ph][:, slot], weight[ph][:, slot], ACT.Exp,
                                     scale=-1.0).then_inc(inv_done, 1)

            def exp_unit(phase, b, first, j):
                ph = late(phase, first, j, 2)
                if ph not in (SPECTRUM, DIFFUSE, MESSAGE):
                    return
                g = count(phase, b, j) - 2
                slot = (j - 2) % RING
                act.wait_ge(sq_done, g + 1)
                nc.scalar.activation(weight[ph][:, slot], weight[ph][:, slot], ACT.Exp,
                                     scale=-2.0).then_inc(exp_done, 1)

            def rstd_start(n, par):
                act.wait_ge(mv_done, n + 1)
                if not isinstance(n, int) or n >= 2:
                    act.wait_ge(rstd_done, n - 1)
                nc.scalar.activation(ln_var[:, par], mv[:, par, :, 1], ACT.Ln,
                                     bias=eps_sb[:, :]).then_inc(lnvar_done, 1)
                act.wait_ge(lnvar_done, n + 1)
                nc.scalar.activation(rstd0[:, par], ln_var[:, par], ACT.Exp, scale=-0.5).then_inc(rstd0_done, 1)

            def period(phase, b, first, j):
                strip = ended_strip(phase, b, first)
                if strip is not None and j == 0:
                    act.wait_ge(spectrum_used, BODY * (strip + 1))
                    nc.scalar.activation(spec_t[:, :, :].rearrange("p t (q j) -> p q t j", q=QUADS),
                                         ps[:, 0:2, :].rearrange("p a (q t j) -> p (a q) t j", q=2, t=TILES),
                                         ACT.Copy).then_inc(spec_copied, 1)
                for ph, chunk, step in tails(phase, b, first, j):
                    n = chunk + (CHUNKS if ph == MESSAGE else 0)
                    if (ph, step) in ((DIFFUSE, 1), (MESSAGE, 4)):
                        par = parity(j, step)
                        if ph == DIFFUSE:
                            act.wait_ge(diffuse_done, GROUPS * STRIPS * (chunk + 1))
                        else:
                            act.wait_ge(message_done, STRIPS * (chunk + 1))
                        act.wait_ge(acc_turned, n)
                        nc.scalar.activation(acc_t[:, :], ps[:, par, :], ACT.Copy).then_inc(acc_copied, 1)
                    if (ph, step) == (DIFFUSE, 4):
                        par = parity(j, step)
                        act.wait_ge(h2_turned, chunk + 1)
                        nc.scalar.activation(
                            h2_t[:, :, :].rearrange("p t (a q j) -> p a q t j", a=2, q=2)[:, par],
                            ps[:, tail_bank(ph, par), :].rearrange("p (q t j) -> p q t j", q=2, t=TILES), ACT.Relu).then_inc(h2t_ready, 1)
                    if (ph, step) == (MESSAGE, 6):
                        act.wait_ge(out_ready, chunk + 1)
                        act.dma_start(out_chunks[chunk], x[:, chunk]).then_inc(out_stored, 16)
                copy_unit(phase, b, first, j)
                ln_unit(phase, b, first, j)
                square_unit(phase, b, first, j)
                inv_unit(phase, b, first, j)
                exp_unit(phase, b, first, j)
                if phase == DIFFUSE:
                    mag_unit(phase, b, first, j)
                for ph, chunk, step in tails(phase, b, first, j):
                    if (ph, step) == (DIFFUSE, 2):
                        rstd_start(CHUNKS + chunk, parity(j, step))
                if phase == SPECTRUM and first and j + 2 < CHUNKS:
                    rstd_start(j + 2, j % 2)

            for k in range(STRIPS):
                act.dma_start(ev_rows[k * TILES:(k + 1) * TILES, :].rearrange("t (q j) -> t q j", q=QUADS),
                              ev_quads[k]).then_inc(small_here, 16)
            act.dma_start(t_sb[:, :], t_in.partition_broadcast(P)).then_inc(small_here, 16)
            act.dma_start(w_sb[:, :], w_in).then_inc(small_here, 16)
            act.dma_start(b_sb[:, :], b_in.partition_broadcast(P)).then_inc(small_here, 16)
            nc.scalar.preload_act_table_set("natural_log_exp_and_others")
            act.wait_ge(eps_ready, 2)
            rstd_start(0, 0)
            act.wait_ge(ev_transposed, 1)
            act.wait_ge(t_ready, 1)
            nc.scalar.activation(coef[:, :], ps[:, 2, 0:N // P], ACT.Exp, scale=t_neg[:, :]).then_inc(coef_ready, 1)
            rstd_start(1, 1)
            bodies(act, SPECTRUM, period)
            bodies(act, DIFFUSE, period)
            bodies(act, MESSAGE, period)
            bodies(act, DRAIN, period, 7)
            act.wait_ge(out_stored, 16 * CHUNKS)

        @block.vector
        def _(dve):
            def diffuse_turn(b, first, j, q):
                u = BODY * b + j
                if q == 0:
                    dve.wait_ge(unit_here[j % RING],
                                16 * (LOADS + QUADS * (BODY // RING * b + j // RING + 1)))
                if not (first and j < 2):
                    dve.wait_ge(diffuse_done, GROUPS * (u - 2) + q + 1)
                if q * 2 == FIRST_W[DIFFUSE] and not (first and j < 2):
                    dve.wait_ge(z_done, UNITS + u - 1)
                src = unit_quads[:, j % RING, :, 2 * q * B32:(2 * q + 2) * B32].rearrange("p r (t i) -> p t r i", t=2)
                dst = adj_t[:, j % 2, 2 * q:2 * q + 2, :].rearrange("p t (r i) -> p t r i", i=B32)
                nc.vector.transpose(dst, src).then_inc(diffuse_turned, 1)

            def message_turn(b, first, j):
                dve.wait_ge(unit_here[j % RING],
                            16 * (LOADS + QUADS * (LOADS + BODY // RING * b + j // RING + 1)))
                if first and j < 2:
                    dve.wait_ge(diffuse_done, GROUPS * (UNITS - 1 + j))
                dve.wait_ge(z_done, 2 * UNITS + BODY * b + j - 1)
                for q in range(N_W[MESSAGE] // 2):
                    src = unit_msg[:, j % RING, :, 2 * q * B32:(2 * q + 2) * B32]\
                        .rearrange("p r (t i) -> p t r i", t=2)
                    dst = adj_t[:, j % 2, 2 * q:2 * q + 2, :].rearrange("p t (r i) -> p t r i", i=B32)
                    last = nc.vector.transpose(dst, src)
                last.then_inc(message_turned, 1)

            def mag_unit(phase, b, first, j):
                u = BODY * b + j
                dst = mag[phase][:, j % RING]
                if not (phase == SPECTRUM and first and j < RING):
                    dve.wait_ge(weight_done, count(phase, b, j) - RING + 1)
                if phase == SPECTRUM:
                    dve.wait_ge(unit_here[j % RING], 16 * (BODY // RING * b + j // RING + 1))
                    dst = dst.rearrange("p (t bq j) -> p t bq j", t=N_W[SPECTRUM], j=B32)
                    src = unit_tiles[:, j % RING, 0:N_W[SPECTRUM]]
                else:
                    dve.wait_ge(message_turned, u + 1)
                    if first and j == 0:
                        dve.wait_ge(diffuse_done, GROUPS * UNITS)
                    src = from_adj(phase)[:, j % 2]
                nc.vector.tensor_scalar(dst.bitcast(mybir.dt.int32), src.bitcast(mybir.dt.int32), SIGN_OFF, None,
                                        ALU.bitwise_and).then_inc(mag_done, 1)

            def z_unit(phase, b, first, j):
                ph = late(phase, first, j, 1)
                if ph not in (SPECTRUM, DIFFUSE, MESSAGE):
                    return
                g, slot = count(phase, b, j) - 1, (j - 1) % RING
                dve.wait_ge(inv_done, g + 1)
                if ph == SPECTRUM:
                    rows = [(unit_tiles[:, slot, t],
                             *(buf[ph][:, slot, t * ROWS:(t + 1) * ROWS].rearrange("p (bq j) -> p bq j", j=B32)
                               for buf in (mag, weight))) for t in range(N_W[SPECTRUM])]
                else:
                    rows = [(from_adj(ph)[:, (j - 1) % 2], mag[ph][:, slot], weight[ph][:, slot])]
                for r, z, inv in rows:
                    last = nc.vector.scalar_tensor_tensor(out=z, in0=r, scalar=1.0, in1=inv, op0=ALU.subtract,
                                                          op1=ALU.mult)
                last.then_inc(z_done, 1)

            def mask_unit(phase, b, first, j):
                ph = late(phase, first, j, 3)
                if ph not in (SPECTRUM, DIFFUSE, MESSAGE):
                    return
                g, slot = count(phase, b, j) - 3, (j - 3) % RING
                dve.wait_ge(exp_done, g + 1)
                nc.vector.scalar_tensor_tensor(out=weight[ph][:, slot], in0=mag[ph][:, slot], scalar=0.0,
                                               in1=weight[ph][:, slot], op0=ALU.is_lt,
                                               op1=ALU.mult).then_inc(weight_done, 1)

            def ln_stats(n, par, rows):
                nc.vector.memset(newton[:, par, 1:2], 0.0)
                for i in range(BLOCKS):
                    last = nc.vector.bn_stats(bn[:, par, i], rows[:, i])
                last.then_inc(bn_done, 1)
                dve.wait_ge(bn_done, n + 1)
                nc.vector.memset(newton[:, par, 0:1], 0.0)
                for i in range(BLOCKS):
                    last = nc.vector.bn_aggr(mv[:, par, i], bn[:, par, i])
                last.then_inc(mv_done, 1)

            def ln_apply(n, par, rows, centred):
                dve.wait_ge(rstd0_done, n + 1)
                nc.vector.tensor_tensor(newton[:, par], rstd0[:, par], rstd0[:, par], ALU.mult).then_inc(nr1_done, 1)
                dve.wait_ge(nr1_done, n + 1)
                nc.vector.scalar_tensor_tensor(out=newton[:, par], in0=mv[:, par, :, 1], scalar=EPS,
                                               in1=newton[:, par], op0=ALU.add, op1=ALU.mult).then_inc(nr2_done, 1)
                dve.wait_ge(nr2_done, n + 1)
                nc.vector.tensor_scalar(newton[:, par], newton[:, par], -0.5, 1.5, ALU.mult, ALU.add)\
                    .then_inc(nr3_done, 1)
                dve.wait_ge(nr3_done, n + 1)
                nc.vector.tensor_tensor(rstd[:, par], newton[:, par], rstd0[:, par], ALU.mult).then_inc(rstd_done, 1)
                dve.wait_ge(rstd_done, n + 1)
                for i in range(BLOCKS):
                    last = nc.vector.tensor_scalar(centred[:, i], rows[:, i], mv[:, par, i, 0:1],
                                                   rstd[:, par, i:i + 1], ALU.subtract, ALU.mult)
                last.then_inc(centred_done, 1)

            def ln_x_stats(c):
                dve.wait_ge(x_here[c], 16)
                ln_stats(c, c % 2, x[:, c])

            def ln_x_apply(c):
                ln_apply(c, c % 2, x[:, c], h[:, c])
                dve.wait_ge(centred_done, c + 1)
                nc.vector.tensor_scalar(h[:, c], h[:, c], 0.0, None, ALU.max).then_inc(h_ready, 1)

            def period(phase, b, first, j):
                strip = ended_strip(phase, b, first)
                if strip is not None and j == 2:
                    dve.wait_ge(spec_turned, strip + 1)
                    dve.wait_ge(coef_ready, 1)
                    nc.vector.tensor_tensor(
                        s[:, bass.ds(strip * TILES, TILES), :],
                        ps[:, 2:4, :].rearrange("p a (t c) -> p (a t) c", c=C),
                        coef[:, bass.ds(strip * TILES, TILES)].unsqueeze(2).broadcast_to([P, TILES, C]),
                        ALU.mult).then_inc(s_ready, 1)
                for ph, chunk, step in tails(phase, b, first, j):
                    par = parity(j, step)
                    bank = ps[:, tail_bank(ph, par), :].rearrange("p (b c) -> p b c", c=C)
                    if (ph, step) == (DIFFUSE, 2):
                        dve.wait_ge(acc_turned, chunk + 1)
                        nc.vector.tensor_tensor(x[:, chunk], x[:, chunk], bank, ALU.add).then_inc(x1_ready, 1)
                        dve.wait_ge(x1_ready, chunk + 1)
                        ln_stats(CHUNKS + chunk, par, x[:, chunk])
                    if (ph, step) == (DIFFUSE, 3):
                        dve.wait_ge(h2_turned, chunk)
                        ln_apply(CHUNKS + chunk, par, x[:, chunk], h2)
                    if (ph, step, par) == (DIFFUSE, 5, 1):
                        k = strip_of(phase, b, first, j, step)
                        dve.wait_ge(msg_summed, k + 1)
                        nc.vector.tensor_tensor(msg[:, bass.ds(k * TILES, TILES), :],
                                                ps[:, 4:6, :].rearrange("p a (t c) -> p (a t) c", c=C),
                                                b_sb[:, :].unsqueeze(1).broadcast_to([P, TILES, C]),
                                                ALU.add).then_inc(msg_ready, 1)
                    if (ph, step) == (MESSAGE, 5):
                        dve.wait_ge(acc_turned, CHUNKS + chunk + 1)
                        nc.vector.tensor_tensor(x[:, chunk], x[:, chunk], bank, ALU.add).then_inc(out_ready, 1)
                if phase == DIFFUSE:
                    diffuse_turn(b, first, j, 0)
                    diffuse_turn(b, first, j, 1)
                    z_unit(phase, b, first, j)
                    diffuse_turn(b, first, j, 2)
                    mask_unit(phase, b, first, j)
                    diffuse_turn(b, first, j, 3)
                    return
                if phase == MESSAGE:
                    message_turn(b, first, j)
                mask_unit(phase, b, first, j)
                if phase != DRAIN:
                    mag_unit(phase, b, first, j)
                if phase == SPECTRUM and first and j + 1 < CHUNKS:
                    ln_x_apply(j + 1)
                z_unit(phase, b, first, j)
                if phase == SPECTRUM and first and j + 2 < CHUNKS:
                    ln_x_stats(j + 2)

            ln_x_stats(0)
            ln_x_stats(1)
            ln_x_apply(0)
            dve.wait_ge(small_here, 16 * (STRIPS + 3))
            nc.vector.tensor_scalar(t_neg[:, :], t_sb[:, :], T_MIN, -1.0, ALU.max, ALU.mult).then_inc(t_ready, 1)
            bodies(dve, SPECTRUM, period)
            bodies(dve, DIFFUSE, period)
            bodies(dve, MESSAGE, period)
            bodies(dve, DRAIN, period, 7)

        @block.tensor
        def _(pe):
            def turn_unit(phase, b, first, j):
                if late(phase, first, j, 4) != SPECTRUM:
                    return
                jj = (j - 4) % BODY
                bb = b if j >= 4 else (BODIES - 1 if first else b - 1)
                pe.wait_ge(weight_done, BODY * bb + jj + 1)
                if not (phase == SPECTRUM and first and j < 6):
                    pe.wait_ge(copied, BODY * bb + jj - 1)
                for t in range(N_W[SPECTRUM]):
                    for i in range(BLOCKS):
                        at = t * ROWS + i * P
                        last = nc.tensor.transpose(ps[:, 4 + 2 * (jj % 2) + t, i * P:(i + 1) * P],
                                                   weight[SPECTRUM][:, jj % RING, at:at + P], ident[:, :])
                last.then_inc(turned, 1)

            def spectrum_period(phase, b, first, j):
                pe.wait_ge(unit_here[j % RING], 16 * (BODY // RING * b + j // RING + 1))
                turn_unit(phase, b, first, j)
                if first:
                    pe.wait_ge(h_ready, j + 1)
                elif j == 0:
                    pe.wait_ge(spec_copied, b)
                for i in range(BLOCKS):
                    for half in range(2):
                        last = nc.tensor.matmul(ps[:, half, :], h[:, j, i, :],
                                                unit_full[:, j % RING, i, half * 512:(half + 1) * 512],
                                                start=(j == 0 and i == 0), stop=(j == BODY - 1 and i == BLOCKS - 1))
                last.then_inc(spectrum_used, 1)
                strip_tail(phase, b, first, j)

            def strip_tail(phase, b, first, j):
                strip = ended_strip(phase, b, first)
                if strip is None or j != 1:
                    return
                pe.wait_ge(spec_copied, strip + 1)
                pe.wait_ge(coef_ready, 1)
                for t in range(TILES):
                    last = nc.tensor.transpose(ps[:, 2 + t // 4, (t % 4) * P:(t % 4 + 1) * P],
                                               spec_t[:, t, :], ident[:, :])
                last.then_inc(spec_turned, 1)

            def diffuse_sum(b, first, j, q):
                u = BODY * b + j
                strip = j % STRIPS
                acc = j // STRIPS
                pe.wait_ge(diffuse_turned, GROUPS * u + q + 1)
                if q == 0 and first and j == 0:
                    pe.wait_ge(spec_copied, STRIPS)
                if q == 0 and first and j < STRIPS:
                    pe.wait_ge(s_ready, strip + 1)
                if q == 0 and strip == 0 and not first:
                    pe.wait_ge(acc_copied, 2 * b + acc - 1)
                for t in range(2):
                    tile = 2 * q + t
                    last = nc.tensor.matmul(ps[:, acc, :], s[:, strip * TILES + tile, :], adj_t[:, j % 2, tile, :],
                                            start=(strip == 0 and tile == 0),
                                            stop=(strip == STRIPS - 1 and tile == TILES - 1))
                last.then_inc(diffuse_done, 1)

            def turn_acc(ph, chunk, bank):
                n = chunk + (CHUNKS if ph == MESSAGE else 0)
                pe.wait_ge(acc_copied, n + 1)
                for i in range(BLOCKS):
                    last = nc.tensor.transpose(ps[:, bank, i * P:(i + 1) * P], acc_t[:, i * P:(i + 1) * P],
                                               ident[:, :])
                last.then_inc(acc_turned, 1)

            def chunk_tails(phase, b, first, j):
                for ph, chunk, step in tails(phase, b, first, j):
                    par = parity(j, step)
                    bank = tail_bank(ph, par)
                    if (ph, step) == (DIFFUSE, 1):
                        if first and ph == phase:
                            pe.wait_ge(s_ready, STRIPS)
                        turn_acc(ph, chunk, bank)
                    if (ph, step) == (DIFFUSE, 3):
                        pe.wait_ge(centred_done, CHUNKS + chunk + 1)
                        for i in range(BLOCKS):
                            last = nc.tensor.transpose(ps[:, bank, i * P:(i + 1) * P], h2[:, i], ident[:, :])
                        last.then_inc(h2_turned, 1)
                    if (ph, step, par) == (DIFFUSE, 4, 1):
                        k = strip_of(phase, b, first, j, step)
                        pe.wait_ge(h2t_ready, chunk + 1)
                        if ph == phase and first:
                            pe.wait_ge(copied, UNITS)
                        for t in range(TILES):
                            last = nc.tensor.matmul(ps[:, 4 + t // 4, (t % 4) * P:(t % 4 + 1) * P],
                                                    h2_t[:, t, :],
                                                    w_sb[:, :], start=True, stop=True)
                        last.then_inc(msg_summed, 1)
                    if (ph, step) == (MESSAGE, 4):
                        turn_acc(ph, chunk, bank)

            def diffuse_period(phase, b, first, j):
                turn_unit(phase, b, first, j)
                for q in range(GROUPS):
                    diffuse_sum(b, first, j, q)
                    if q == 1:
                        strip_tail(phase, b, first, j)
                        chunk_tails(phase, b, first, j)

            def message_sum(phase, b, first, j):
                ph = late(phase, first, j, MSG_LAG)
                if ph != MESSAGE:
                    return
                g = count(phase, b, j) - MSG_LAG
                jj = (j - MSG_LAG) % BODY
                bb = b if j >= MSG_LAG else (BODIES - 1 if first else b - 1)
                strip, acc, slot = jj % STRIPS, jj // STRIPS, jj % RING
                if strip == 0:
                    if first and phase == MESSAGE:
                        pe.wait_ge(acc_copied, CHUNKS - 1)
                    else:
                        pe.wait_ge(acc_copied, CHUNKS)
                if first and phase == MESSAGE:
                    pe.wait_ge(msg_ready, strip + 1)
                pe.wait_ge(w_here[slot], 16 * (BODY // RING * bb + jj // RING + 1))
                for t in range(STORED):
                    nc.tensor.matmul(ps[:, acc, :], msg[:, strip * TILES + t, :], w_back[:, slot, t, :],
                                     start=(strip == 0 and t == 0), stop=False)
                pe.wait_ge(weight_done, g + 1)
                for t in range(STORED, TILES):
                    last = nc.tensor.matmul(ps[:, acc, :], msg[:, strip * TILES + t, :],
                                            weight[MESSAGE][:, slot, (t - STORED) * ROWS:(t - STORED + 1) * ROWS],
                                            start=False, stop=(strip == STRIPS - 1 and t == TILES - 1))
                last.then_inc(message_done, 1)

            def message_period(phase, b, first, j):
                message_sum(phase, b, first, j)
                chunk_tails(phase, b, first, j)

            def drain_period(phase, b, first, j):
                message_sum(phase, b, first, j)
                chunk_tails(phase, b, first, j)

            pe.wait_ge(ident_ready, 2)
            pe.wait_ge(small_here, 16 * (STRIPS + 3))
            nc.tensor.transpose(ps[:, 2, 0:N // P], ev_rows[:, :], ident[0:N // P, 0:N // P])\
                .then_inc(ev_transposed, 1)
            bodies(pe, SPECTRUM, spectrum_period)
            bodies(pe, DIFFUSE, diffuse_period)
            bodies(pe, MESSAGE, message_period)
            bodies(pe, DRAIN, drain_period, 7)


_INS = ["x", "adj", "L0_gnn_evals", "L0_gnn_t", "L1_gnn_W", "L1_gnn_B"]


def kernel(**inputs):
    import numpy as _np
    import concourse.bacc as _bacc
    from concourse import mybir as _mybir
    from concourse.bass_utils import run_bass_kernel_spmd as _run

    nc = _bacc.Bacc("TRN2", target_bir_lowering=False, num_devices=1)
    arrays, args = {}, []
    for name in _INS:
        a = _np.ascontiguousarray(inputs[name])
        arrays[f"in_{name}_dram"] = a
        args.append(nc.dram_tensor(f"in_{name}_dram", a.shape, _mybir.dt.from_np(a.dtype), kind="ExternalInput").ap())
    rows, cols = arrays["in_x_dram"].shape
    out = nc.dram_tensor("out_dram", (rows, cols), _mybir.dt.float32, kind="ExternalOutput").ap()
    adjacency_diffusion_message_kernel(nc, *args, out)
    r = _run(nc, [arrays], core_ids=[0])
    return r.results[0]["out_dram"]
```

```python
import concourse.bass as bass
from concourse import mybir
from contextlib import ExitStack


def adjacency_diffusion_message_kernel(nc: bass.Bass, x_in: bass.AP, adj: bass.AP, evals: bass.AP, t_in: bass.AP,
                                       w_in: bass.AP, b_in: bass.AP, out: bass.AP):
    fp32 = mybir.dt.float32
    ALU = mybir.AluOpType
    ACT = mybir.ActivationFunctionType

    P = 128
    N, C = x_in.shape
    BLOCKS = 4
    ROWS = BLOCKS * P
    TILES = 8
    COLS = TILES * P
    CHUNKS = N // ROWS
    STRIPS = N // COLS
    UNITS = CHUNKS * STRIPS
    BODY = 8
    BODIES = UNITS // BODY
    SPECTRUM, DIFFUSE, MESSAGE, DRAIN = range(4)
    W_TILES = {SPECTRUM: ((1, 2, 3), (1, 2, 3), (1, 2, 3), (1, 2, 3)),
               DIFFUSE: ((0, 4), (0, 4), (0, 4), (0,)),
               MESSAGE: ((5, 6, 7), (5, 6, 7), (5, 6, 7), (4, 5, 6, 7))}
    TURNED = len(W_TILES[SPECTRUM][0])
    RAW = 4
    GROUPS = TILES // 2
    QUADS = 4
    B32 = 32
    R_BLOCKS = ROWS // B32
    RING = 4
    LOADS = UNITS // RING
    MSG_LAG = 4
    STORED_LAG = 1
    STORED_FIRST = {0: 0, 1: 2, 2: 1, 3: 4, 4: 5, 5: 6, 6: 3}
    LOADED_FIRST = len(STORED_FIRST)
    LN_IN = {0: (1, 2), 1: (3,), 2: (4,), 3: (5,), 4: (6,), 5: (7,)}
    EPS = 1e-5
    T_MIN = 1e-8
    R_TINY = float(2.0 ** -30)
    SIGN_OFF = 0x7FFFFFFF
    assert TILES * B32 * QUADS == COLS and RAW == GROUPS

    def n_w(phase, slot):
        return len(W_TILES[phase][slot % RING])

    def n_stored(slot):
        return TILES - n_w(MESSAGE, slot)

    adj_full = adj.rearrange("(n b p) (k c) -> n k p b c", b=BLOCKS, p=P, c=COLS)
    adj_quads = adj.rearrange("(n r i) (k q c) -> n k q i r c", r=R_BLOCKS, i=B32, q=QUADS, c=COLS // QUADS)
    ev_quads = evals.rearrange("(k q t j) -> k t q j", q=QUADS, t=TILES, j=B32)
    x_chunks = x_in.rearrange("(n b p) c -> n p b c", b=BLOCKS, p=P)
    out_chunks = out.rearrange("(n b p) c -> n p b c", b=BLOCKS, p=P)
    w_dram = nc.dram_tensor("weights_t", [CHUNKS, STRIPS, P, TILES - n_w(MESSAGE, 0), ROWS], fp32).ap()

    ctx = ExitStack()
    with ctx:
        def sb(name, shape):
            return ctx.enter_context(nc.sbuf_tensor(name, shape, fp32))

        def sem(name):
            return ctx.enter_context(nc.semaphore(name))

        unit = sb("unit", [P, RING, BLOCKS * COLS])
        unit_full = unit[:, :, :].rearrange("p r (b c) -> p r b c", b=BLOCKS)
        unit_quads = unit[:, :, :].rearrange("p r (b c) -> p r b c", b=R_BLOCKS)
        E_PART = RAW * ROWS
        unit_msg = unit[:, :, 0:E_PART].rearrange("p r (b c) -> p r b c", b=R_BLOCKS)
        w_back = unit[:, :, E_PART:].rearrange("p r (t n) -> p r t n", t=TILES - RAW)
        x = sb("x", [P, CHUNKS, BLOCKS, C])
        h = sb("h", [P, CHUNKS, BLOCKS, C])
        msg = h[:, :, :, :].rearrange("p n b c -> p (n b) c")
        adj_t = sb("adj_t", [P, 2, TILES, ROWS])
        work = sb("work", [P, 32 * ROWS])
        s = work[:, 0:STRIPS * TILES * C].rearrange("p (t c) -> p t c", c=C)
        assert STRIPS * TILES * C == 8 * ROWS
        STAGE_AT = (8, 11)
        MAG_AT = {SPECTRUM: (None, None, 14, 17), DIFFUSE: (20, 24, 26, 30), MESSAGE: (8, 0, 11, 20)}
        WEIGHT_AT = {SPECTRUM: (20, 23, 26, 29), DIFFUSE: (22, 14, 17, 19), MESSAGE: (4, 24, 14, 28)}

        def work_tiles(at, n):
            return work[:, at * ROWS:(at + n) * ROWS]

        def mag(phase, slot):
            if phase == SPECTRUM and slot < 2:
                return adj_t[:, 1, TURNED * slot:TURNED * (slot + 1), :].rearrange("p t n -> p (t n)")
            return work_tiles(MAG_AT[phase][slot], n_w(phase, slot))

        def weight(phase, slot):
            return work_tiles(WEIGHT_AT[phase][slot], n_w(phase, slot))

        def stage(slot):
            return work_tiles(STAGE_AT[slot], TURNED)

        spec_t = sb("spec_t", [P, TILES, P])
        acc_t = sb("acc_t", [P, ROWS])
        h2 = sb("h2", [P, BLOCKS, C])
        h2_t = sb("h2_t", [P, TILES, P])
        ident = sb("ident", [P, P])
        w_sb = sb("w_sb", [C, C])
        b_sb = sb("b_sb", [P, C])
        ev_rows = sb("ev_rows", [N // P, P])
        t_sb = sb("t_sb", [P, 1])
        t_neg = sb("t_neg", [P, 1])
        coef = sb("coef", [P, N // P])
        bn = sb("bn", [P, 2, BLOCKS, 6])
        mv = sb("mv", [P, 2, BLOCKS, 2])
        ln_var = sb("ln_var", [P, 2, BLOCKS])
        rstd0 = sb("rstd0", [P, 2, BLOCKS])
        newton = sb("newton", [P, 2, BLOCKS])
        rstd = sb("rstd", [P, 2, BLOCKS])
        shift = sb("shift", [P, 2, BLOCKS])
        eps_sb = sb("eps_sb", [P, 1])
        tiny_sb = sb("tiny_sb", [P, 1])

        ps = ctx.enter_context(nc.psum_tensor("ps", [P, 8, 512], fp32))

        x_here = [sem(f"x_here{c}") for c in range(CHUNKS)]
        small_here = sem("small_here")
        ident_ready = sem("ident_ready")
        eps_ready = sem("eps_ready")
        t_ready = sem("t_ready")
        ev_transposed = sem("ev_transposed")
        coef_ready = sem("coef_ready")
        unit_here = [sem(f"unit_here{i}") for i in range(RING)]
        first_here = [sem(f"first_here{i}") for i in range(BLOCKS - 1)]
        spectrum_used = sem("spectrum_used")
        turned = sem("turned")
        copied = sem("copied")
        diffuse_turned = sem("diffuse_turned")
        message_turned = sem("message_turned")
        mag_done = sem("mag_done")
        abs_done = sem("abs_done")
        ln_done = sem("ln_done")
        inv_done = sem("inv_done")
        z_done = sem("z_done")
        sq_done = sem("sq_done")
        exp_done = sem("exp_done")
        weight_done = sem("weight_done")
        w_stored = [sem(f"w_stored{i}") for i in range(RING)]
        w_here = [sem(f"w_here{i}") for i in range(RING)]
        spec_copied = sem("spec_copied")
        spec_turned = sem("spec_turned")
        s_ready = sem("s_ready")
        diffuse_done = sem("diffuse_done")
        stored_used = [sem(f"stored_used{i}") for i in range(RING)]
        message_done = sem("message_done")
        acc_copied = sem("acc_copied")
        acc_turned = sem("acc_turned")
        x1_ready = sem("x1_ready")
        bn_done = sem("bn_done")
        mv_done = sem("mv_done")
        lnvar_done = sem("lnvar_done")
        rstd0_done = sem("rstd0_done")
        nr1_done = sem("nr1_done")
        nr2_done = sem("nr2_done")
        nr3_done = sem("nr3_done")
        rstd_done = sem("rstd_done")
        centred_done = sem("centred_done")
        shift_ready = sem("shift_ready")
        h2_ready = sem("h2_ready")
        h_ready = sem("h_ready")
        h2_turned = sem("h2_turned")
        h2t_ready = sem("h2t_ready")
        msg_summed = sem("msg_summed")
        msg_ready = sem("msg_ready")
        out_ready = sem("out_ready")
        out_stored = sem("out_stored")

        def bodies(eng, phase, period, periods=BODY):
            for j in range(periods):
                period(phase, 0, True, j)
            if phase != DRAIN:
                with eng.Fori(1, BODIES) as b:
                    for j in range(BODY):
                        period(phase, b, False, j)

        def count(phase, b, j):
            return phase * UNITS + BODY * b + j

        def late(phase, first, j, lag):
            return phase - 1 if first and j < lag else phase

        def tails(phase, b, first, j):
            found = [(phase, 2 * b, j - 4)] if phase != DRAIN else []
            if not first:
                found += [(phase, 2 * (b - 1), j + 4), (phase, 2 * (b - 1) + 1, j)]
            elif phase > 0:
                found += [(phase - 1, CHUNKS - 2, j + 4), (phase - 1, CHUNKS - 1, j)]
            return [f for f in found if f[0] in (DIFFUSE, MESSAGE) and f[2] >= 1]

        def ended_strip(phase, b, first):
            if phase == SPECTRUM and not first:
                return b - 1
            if phase == DIFFUSE and first:
                return STRIPS - 1
            return None

        def from_adj(phase, slot):
            if phase == DIFFUSE:
                return adj_t[:, slot % 2, 0:GROUPS * (n_w(phase, slot) - 1) + 1:GROUPS, :]
            return adj_t[:, slot % 2, 0:n_w(phase, slot), :]

        def by_tile(buffer):
            return buffer.rearrange("p (t n) -> p t n", n=ROWS)

        def w_back_last(slot):
            if slot == 1:
                return adj_t[:, 0, TILES - 1, :]
            return spec_t[:, slot // 2 * 4:slot // 2 * 4 + 4, :].rearrange("p t j -> p (t j)")

        unit_tiles = unit[:, :, :].rearrange("p r (bq t j) -> p r t bq j", t=TILES, j=B32)

        def strip_of(b, first):
            return b - 1 if not first else BODIES - 1

        def parity(j, step):
            return 1 if step == j else 0

        def tail_bank(chunk_parity):
            return 2 + chunk_parity

        def ago(b, first, j, lag):
            return (b if j >= lag else BODIES - 1 if first else b - 1), (j - lag) % BODY

        def known_zero(value):
            return isinstance(value, int) and value == 0

        def turn_bank(jj, t):
            return 4 + (TURNED * jj + t) % 4

        block = ctx.enter_context(nc.Block())

        @block.sync
        def _(sp):
            def load_weights(bb, jj):
                if isinstance(bb, int) and bb == 0 and jj == 0:
                    for i in range(RING):
                        sp.wait_ge(w_stored[i], 16 * LOADS)
                if not (isinstance(bb, int) and bb == 0 and jj < RING):
                    sp.wait_ge(stored_used[jj % RING], BODY // RING * bb + jj // RING)
                elif jj == 0:
                    sp.wait_ge(spec_turned, STRIPS)
                sp.wait_ge(x_here[0], 16)
                sp.wait_ge(w_stored[jj % RING], 16 * (LOADS + BODY // RING * bb + jj // RING + 1))
                sp.dma_start(w_back[:, jj % RING], w_dram[2 * bb + jj // STRIPS, jj % STRIPS][:, 0:TILES - RAW, :])\
                    .then_inc(w_here[jj % RING], 16)
                if not (isinstance(bb, int) and bb == 0 and jj == 1):
                    load_fifth(bb, jj)

            def load_fifth(bb, jj):
                if n_stored(jj) > TILES - RAW:
                    sp.dma_start(w_back_last(jj % RING),
                                 w_dram[2 * bb + jj // STRIPS, jj % STRIPS][:, TILES - RAW, :])\
                        .then_inc(w_here[jj % RING], 16)

            def period(phase, b, first, j):
                g = count(phase, b, j)
                u = BODY * b + j
                slot = j % RING
                if late(phase, first, j, 7) == SPECTRUM:
                    jj = (j - 7) % BODY
                    bb = b if j >= 7 else (BODIES - 1 if first else b - 1)
                    sp.wait_ge(copied, TURNED * (BODY * bb + jj + 1))
                    sp.dma_start(w_dram[jj, bb][:, 1:1 + TURNED, :], by_tile(stage(jj % 2)))\
                        .then_inc(w_stored[jj % RING], 16)
                if late(phase, first, j, 7) == DIFFUSE:
                    jj = (j - 7) % BODY
                    bb = b if j >= 7 else (BODIES - 1 if first else b - 1)
                    sp.wait_ge(weight_done, count(DIFFUSE, bb, jj) + 1)
                    tiles = slice(0, GROUPS * (n_w(DIFFUSE, jj) - 1) + 1, GROUPS)
                    sp.dma_start(w_dram[2 * bb + jj // STRIPS, jj % STRIPS][:, tiles, :],
                                 by_tile(weight(DIFFUSE, jj % RING))).then_inc(w_stored[jj % RING], 16)
                if phase != DRAIN:
                    old = late(phase, first, j, RING)
                    if old == SPECTRUM:
                        sp.wait_ge(spectrum_used, g - RING + 1)
                        sp.wait_ge(z_done, g - RING + 1)
                    elif old == DIFFUSE:
                        sp.wait_ge(diffuse_turned, GROUPS * (g - RING - UNITS) + GROUPS)
                    elif old == MESSAGE:
                        sp.wait_ge(message_turned, u - RING + 1)
                    if phase == SPECTRUM:
                        sp.dma_start(unit_full[:, slot], adj_full[j, b]).then_inc(unit_here[slot], 16)
                    else:
                        for q in range(QUADS):
                            src = adj_quads[2 * b + j // STRIPS, j % STRIPS, q]
                            dst = unit_quads if phase == DIFFUSE else unit_msg
                            if phase == MESSAGE:
                                src = src[:, :, (TILES - RAW) * B32:TILES * B32]
                            sp.dma_start(dst[q * B32:(q + 1) * B32, slot], src).then_inc(unit_here[slot], 16)
                if phase == MESSAGE and first:
                    if j < LOADED_FIRST:
                        load_weights(0, j)
                    if j == 3:
                        sp.wait_ge(diffuse_done, GROUPS * (UNITS - 1))
                        load_fifth(0, 1)
                elif late(phase, first, j, STORED_LAG) == MESSAGE:
                    load_weights(*ago(b, first, j, STORED_LAG))

            sp.dma_start(x[:, 0], x_chunks[0]).then_inc(x_here[0], 16)
            for i in range(BLOCKS - 1):
                sp.dma_start(unit_full[:, 0, i], adj_full[0, 0][:, i]).then_inc(first_here[i], 16)
            sp.dma_start(unit_full[:, 0, BLOCKS - 1], adj_full[0, 0][:, BLOCKS - 1]).then_inc(unit_here[0], 16)
            for c in LN_IN[0]:
                sp.dma_start(x[:, c], x_chunks[c]).then_inc(x_here[c], 16)
            for j in range(1, BODY):
                period(SPECTRUM, 0, True, j)
                for c in LN_IN.get(j, ()):
                    sp.dma_start(x[:, c], x_chunks[c]).then_inc(x_here[c], 16)
            with sp.Fori(1, BODIES) as b:
                for j in range(BODY):
                    period(SPECTRUM, b, False, j)
            bodies(sp, DIFFUSE, period)
            bodies(sp, MESSAGE, period)
            bodies(sp, DRAIN, period, 4)

        @block.gpsimd
        def _(pool):
            nc.gpsimd.memset(tiny_sb[:, :], R_TINY).then_inc(eps_ready, 1)
            nc.gpsimd.memset(eps_sb[:, :], EPS).then_inc(eps_ready, 1)
            nc.gpsimd.memset(ident[:, :], 0.0).then_inc(ident_ready, 1)
            pool.wait_ge(ident_ready, 1)
            nc.gpsimd.affine_select(out=ident[:, :], in_=ident[:, :], compare_op=ALU.not_equal, fill=1.0, base=0,
                                    pattern=[[-1, P]], channel_multiplier=1).then_inc(ident_ready, 1)

        @block.scalar
        def _(act):
            def copy_unit(phase, b, first, j):
                if late(phase, first, j, 4) != SPECTRUM:
                    return
                jj = (j - 4) % BODY
                bb = b if j >= 4 else (BODIES - 1 if first else b - 1)
                if not (phase == SPECTRUM and first and j < 6):
                    act.wait_ge(w_stored[(jj - 2) % RING], 16 * (BODY // RING * bb + (jj - 2) // RING + 1))
                for t in range(TURNED):
                    act.wait_ge(turned, TURNED * (BODY * bb + jj) + t + 1)
                    nc.scalar.activation(stage(jj % 2)[:, t * ROWS:(t + 1) * ROWS], ps[:, turn_bank(jj, t), :],
                                         ACT.Copy).then_inc(copied, 1)

            def mag_unit(phase, b, first, j):
                u = BODY * b + j
                act.wait_ge(diffuse_turned, GROUPS * u + 1)
                if first and j < RING:
                    act.wait_ge(turned, TURNED * (UNITS - RING + j + 1))
                else:
                    act.wait_ge(weight_done, UNITS + u - RING + 1)
                nc.scalar.activation(by_tile(mag(DIFFUSE, j % RING)), from_adj(DIFFUSE, j),
                                     ACT.Abs).then_inc(abs_done, 1)

            def ln_unit(phase, b, first, j):
                ph = late(phase, first, j, 1)
                if ph not in (SPECTRUM, DIFFUSE, MESSAGE):
                    return
                g = count(phase, b, j) - 1
                slot = (j - 1) % RING
                if ph == SPECTRUM:
                    act.wait_ge(mag_done, g + 1)
                elif ph == DIFFUSE:
                    act.wait_ge(abs_done, g - UNITS + 1)
                else:
                    act.wait_ge(mag_done, g - UNITS + 1)
                old = late(phase, first, j, 1 + RING)
                bb = b if j >= 1 + RING else (b - 1 if not first else BODIES - 1)
                loads = BODY // RING * bb + ((j - 1 - RING) % BODY) // RING + 1
                if ph == old == SPECTRUM:
                    act.wait_ge(turned, TURNED * (g - RING + 1))
                elif ph == old == DIFFUSE:
                    act.wait_ge(w_stored[slot], 16 * (LOADS + loads))
                elif old == SPECTRUM:
                    if slot == 0:
                        act.wait_ge(turned, TURNED * (UNITS - 2))
                    else:
                        act.wait_ge(weight_done, UNITS - 1 if slot == 1 else UNITS)
                elif old == DIFFUSE and slot == 0:
                    act.wait_ge(diffuse_done, GROUPS * UNITS)
                elif old == DIFFUSE and slot == 1:
                    act.wait_ge(weight_done, 2 * UNITS - 1)
                elif old == DIFFUSE and slot == 2:
                    act.wait_ge(w_stored[1], 16 * 2 * LOADS)
                elif old == DIFFUSE:
                    act.wait_ge(weight_done, 2 * UNITS)
                elif old == MESSAGE:
                    act.wait_ge(message_done, g - RING - MESSAGE * UNITS + 1)
                nc.scalar.activation(weight(ph, slot), mag(ph, slot), ACT.Ln,
                                     bias=tiny_sb[:, :]).then_inc(ln_done, 1)

            def square_unit(phase, b, first, j):
                ph = late(phase, first, j, 2)
                if ph not in (SPECTRUM, DIFFUSE, MESSAGE):
                    return
                g = count(phase, b, j) - 2
                slot = (j - 2) % RING
                act.wait_ge(z_done, g + 1)
                nc.scalar.activation(weight(ph, slot), mag(ph, slot), ACT.Square).then_inc(sq_done, 1)

            def inv_unit(phase, b, first, j):
                ph = late(phase, first, j, 1)
                if ph not in (SPECTRUM, DIFFUSE, MESSAGE):
                    return
                g = count(phase, b, j) - 1
                slot = (j - 1) % RING
                act.wait_ge(ln_done, g + 1)
                nc.scalar.activation(weight(ph, slot), weight(ph, slot), ACT.Exp,
                                     scale=-1.0).then_inc(inv_done, 1)

            def exp_unit(phase, b, first, j):
                ph = late(phase, first, j, 2)
                if ph not in (SPECTRUM, DIFFUSE, MESSAGE):
                    return
                g = count(phase, b, j) - 2
                slot = (j - 2) % RING
                act.wait_ge(sq_done, g + 1)
                nc.scalar.activation(weight(ph, slot), weight(ph, slot), ACT.Exp,
                                     scale=-2.0).then_inc(exp_done, 1)

            def rstd_start(n, par):
                act.wait_ge(mv_done, n + 1)
                if not isinstance(n, int) or n >= 2:
                    act.wait_ge(rstd_done, n - 1)
                nc.scalar.activation(ln_var[:, par], mv[:, par, :, 1], ACT.Ln,
                                     bias=eps_sb[:, :]).then_inc(lnvar_done, 1)
                act.wait_ge(lnvar_done, n + 1)
                nc.scalar.activation(rstd0[:, par], ln_var[:, par], ACT.Exp, scale=-0.5).then_inc(rstd0_done, 1)

            def period(phase, b, first, j):
                strip = ended_strip(phase, b, first)
                if strip is not None and j == 0:
                    act.wait_ge(spectrum_used, BODY * (strip + 1))
                    nc.scalar.activation(spec_t[:, :, :].rearrange("p t (q j) -> p q t j", q=QUADS),
                                         ps[:, 0:2, :].rearrange("p a (q t j) -> p (a q) t j", q=2, t=TILES),
                                         ACT.Copy).then_inc(spec_copied, 1)
                for ph, chunk, step in tails(phase, b, first, j):
                    n = chunk + (CHUNKS if ph == MESSAGE else 0)
                    if (ph, step) in ((DIFFUSE, 1), (MESSAGE, 4)):
                        par = parity(j, step)
                        if ph == DIFFUSE:
                            act.wait_ge(diffuse_done, GROUPS * STRIPS * (chunk + 1))
                        else:
                            act.wait_ge(message_done, STRIPS * (chunk + 1))
                        if not known_zero(n):
                            act.wait_ge(acc_turned, n)
                        nc.scalar.activation(acc_t[:, :], ps[:, par, :], ACT.Copy).then_inc(acc_copied, 1)
                    if (ph, step) == (DIFFUSE, 3):
                        par = parity(j, step)
                        act.wait_ge(shift_ready, chunk + 1)
                        if not known_zero(chunk):
                            act.wait_ge(h2_turned, chunk)
                        for i in range(BLOCKS):
                            last = nc.scalar.activation(h2[:, i], x[:, chunk, i], ACT.Identity,
                                                        bias=shift[:, par, i:i + 1], scale=rstd[:, par, i:i + 1])
                        last.then_inc(h2_ready, 1)
                    if (ph, step) == (DIFFUSE, 4):
                        par = parity(j, step)
                        act.wait_ge(h2_turned, chunk + 1)
                        nc.scalar.activation(
                            h2_t[:, :, :].rearrange("p t (a q j) -> p a q t j", a=2, q=2)[:, par],
                            ps[:, tail_bank(par), :].rearrange("p (q t j) -> p q t j", q=2, t=TILES),
                            ACT.Relu).then_inc(h2t_ready, 1)
                    if (ph, step) == (MESSAGE, 6):
                        act.wait_ge(out_ready, chunk + 1)
                        act.dma_start(out_chunks[chunk], x[:, chunk]).then_inc(out_stored, 16)
                if phase == SPECTRUM:
                    copy_unit(phase, b, first, j)
                ln_unit(phase, b, first, j)
                square_unit(phase, b, first, j)
                inv_unit(phase, b, first, j)
                exp_unit(phase, b, first, j)
                if phase == DIFFUSE:
                    mag_unit(phase, b, first, j)
                    copy_unit(phase, b, first, j)
                for ph, chunk, step in tails(phase, b, first, j):
                    if (ph, step) == (DIFFUSE, 2):
                        rstd_start(CHUNKS + chunk, parity(j, step))
                if phase == SPECTRUM and first:
                    for c in LN_IN.get(j, ()):
                        rstd_start(c, c % 2)
                if phase == SPECTRUM and first and j == 5:
                    act.wait_ge(ev_transposed, 1)
                    act.wait_ge(t_ready, 1)
                    nc.scalar.activation(coef[:, :], ps[:, 2, 0:N // P], ACT.Exp, scale=t_neg[:, :])\
                        .then_inc(coef_ready, 1)

            nc.scalar.preload_act_table_set("natural_log_exp_and_others")
            act.wait_ge(eps_ready, 2)
            rstd_start(0, 0)
            for k in range(STRIPS):
                act.dma_start(ev_rows[k * TILES:(k + 1) * TILES, :].rearrange("t (q j) -> t q j", q=QUADS),
                              ev_quads[k]).then_inc(small_here, 16)
            act.dma_start(t_sb[:, :], t_in.partition_broadcast(P)).then_inc(small_here, 16)
            act.dma_start(w_sb[:, :], w_in).then_inc(small_here, 16)
            act.dma_start(b_sb[:, :], b_in.partition_broadcast(P)).then_inc(small_here, 16)
            bodies(act, SPECTRUM, period)
            bodies(act, DIFFUSE, period)
            bodies(act, MESSAGE, period)
            bodies(act, DRAIN, period, 7)
            act.wait_ge(out_stored, 16 * CHUNKS)

        @block.vector
        def _(dve):
            def diffuse_turn(b, first, j, q):
                u = BODY * b + j
                if q == 0:
                    dve.wait_ge(unit_here[j % RING],
                                16 * (LOADS + QUADS * (BODY // RING * b + j // RING + 1)))
                if not (first and j < 2):
                    dve.wait_ge(diffuse_done, GROUPS * (u - 2) + q + 1)
                if q == 0 and first and j == 1:
                    dve.wait_ge(weight_done, UNITS - 2)
                if q == 0 and not (first and j < 2):
                    dve.wait_ge(z_done, UNITS + u - 1)
                src = unit_quads[:, j % RING].rearrange("p r (h q i) -> p q h r i", h=2, i=B32)[:, q]
                dst = adj_t[:, j % 2].rearrange("p (h q) (r i) -> p q h r i", h=2, i=B32)[:, q]
                nc.vector.transpose(dst, src).then_inc(diffuse_turned, 1)

            def message_turn(b, first, j):
                dve.wait_ge(unit_here[j % RING],
                            16 * (LOADS + QUADS * (LOADS + BODY // RING * b + j // RING + 1)))
                if first and j < 2:
                    dve.wait_ge(diffuse_done, GROUPS * (UNITS - 1 + j))
                dve.wait_ge(z_done, 2 * UNITS + BODY * b + j - 1)
                nc.vector.transpose(
                    from_adj(MESSAGE, j).rearrange("p t (r i) -> p t r i", i=B32),
                    unit_msg[:, j % RING, :, (RAW - n_w(MESSAGE, j)) * B32:]
                    .rearrange("p r (t i) -> p t r i", i=B32)).then_inc(message_turned, 1)

            def mag_unit(phase, b, first, j):
                u = BODY * b + j
                dst = mag(phase, j % RING)
                if not (phase == SPECTRUM and first and j < RING):
                    dve.wait_ge(weight_done, count(phase, b, j) - RING + 1)
                if phase == SPECTRUM:
                    if first and j == 0:
                        for i in range(BLOCKS - 1):
                            dve.wait_ge(first_here[i], 16)
                    dve.wait_ge(unit_here[j % RING], 16 * (BODY // RING * b + j // RING + 1))
                    dst = dst.rearrange("p (t bq j) -> p t bq j", t=TURNED, j=B32)
                    src = unit_tiles[:, j % RING, 1:1 + TURNED]
                else:
                    dve.wait_ge(message_turned, u + 1)
                    if first and j in (0, 2):
                        for i in range(RING):
                            dve.wait_ge(w_stored[i], 16 * LOADS)
                    if first and j == 1:
                        dve.wait_ge(diffuse_done, GROUPS * UNITS)
                    if first and j == 3:
                        dve.wait_ge(w_stored[0], 16 * 2 * LOADS)
                    src = from_adj(phase, j)
                    dst = by_tile(dst)
                nc.vector.tensor_scalar(dst.bitcast(mybir.dt.int32), src.bitcast(mybir.dt.int32), SIGN_OFF, None,
                                        ALU.bitwise_and).then_inc(mag_done, 1)

            def z_unit(phase, b, first, j):
                ph = late(phase, first, j, 1)
                if ph not in (SPECTRUM, DIFFUSE, MESSAGE):
                    return
                g, slot = count(phase, b, j) - 1, (j - 1) % RING
                dve.wait_ge(inv_done, g + 1)
                if ph == SPECTRUM:
                    rows = [(unit_tiles[:, slot, 1 + t],
                             *(buf(ph, slot)[:, t * ROWS:(t + 1) * ROWS].rearrange("p (bq j) -> p bq j", j=B32)
                               for buf in (mag, weight))) for t in range(TURNED)]
                else:
                    rows = [(from_adj(ph, slot), by_tile(mag(ph, slot)), by_tile(weight(ph, slot)))]
                for r, z, inv in rows:
                    last = nc.vector.scalar_tensor_tensor(out=z, in0=r, scalar=1.0, in1=inv, op0=ALU.subtract,
                                                          op1=ALU.mult)
                last.then_inc(z_done, 1)

            def mask_unit(phase, b, first, j):
                ph = late(phase, first, j, 3)
                if ph not in (SPECTRUM, DIFFUSE, MESSAGE):
                    return
                g, slot = count(phase, b, j) - 3, (j - 3) % RING
                dve.wait_ge(exp_done, g + 1)
                nc.vector.scalar_tensor_tensor(out=weight(ph, slot), in0=mag(ph, slot), scalar=0.0,
                                               in1=weight(ph, slot), op0=ALU.is_lt,
                                               op1=ALU.mult).then_inc(weight_done, 1)

            def ln_stats(n, par, rows):
                nc.vector.memset(newton[:, par, 1:2], 0.0)
                for i in range(BLOCKS):
                    last = nc.vector.bn_stats(bn[:, par, i], rows[:, i])
                last.then_inc(bn_done, 1)
                dve.wait_ge(bn_done, n + 1)
                nc.vector.memset(newton[:, par, 0:1], 0.0)
                for i in range(BLOCKS):
                    last = nc.vector.bn_aggr(mv[:, par, i], bn[:, par, i])
                last.then_inc(mv_done, 1)

            def ln_newton(n, par):
                dve.wait_ge(rstd0_done, n + 1)
                nc.vector.tensor_tensor(newton[:, par], rstd0[:, par], rstd0[:, par], ALU.mult).then_inc(nr1_done, 1)
                dve.wait_ge(nr1_done, n + 1)
                nc.vector.scalar_tensor_tensor(out=newton[:, par], in0=mv[:, par, :, 1], scalar=EPS,
                                               in1=newton[:, par], op0=ALU.add, op1=ALU.mult).then_inc(nr2_done, 1)
                dve.wait_ge(nr2_done, n + 1)
                nc.vector.tensor_scalar(newton[:, par], newton[:, par], -0.5, 1.5, ALU.mult, ALU.add)\
                    .then_inc(nr3_done, 1)
                dve.wait_ge(nr3_done, n + 1)
                nc.vector.tensor_tensor(rstd[:, par], newton[:, par], rstd0[:, par], ALU.mult).then_inc(rstd_done, 1)
                dve.wait_ge(rstd_done, n + 1)

            def ln_x_stats(c):
                dve.wait_ge(x_here[c], 16)
                ln_stats(c, c % 2, x[:, c])

            def ln_x_apply(c):
                ln_newton(c, c % 2)
                for i in range(BLOCKS):
                    last = nc.vector.tensor_scalar(h[:, c, i], x[:, c, i], mv[:, c % 2, i, 0:1],
                                                   rstd[:, c % 2, i:i + 1], ALU.subtract, ALU.mult)
                last.then_inc(centred_done, 1)
                dve.wait_ge(centred_done, c + 1)
                nc.vector.tensor_scalar(h[:, c], h[:, c], 0.0, None, ALU.max).then_inc(h_ready, 1)

            def period(phase, b, first, j):
                strip = ended_strip(phase, b, first)
                if strip is not None and j == 2:
                    dve.wait_ge(spec_turned, strip + 1)
                    dve.wait_ge(coef_ready, 1)
                    nc.vector.tensor_tensor(
                        s[:, bass.ds(strip * TILES, TILES), :],
                        ps[:, 2:4, :].rearrange("p a (t c) -> p (a t) c", c=C),
                        coef[:, bass.ds(strip * TILES, TILES)].unsqueeze(2).broadcast_to([P, TILES, C]),
                        ALU.mult).then_inc(s_ready, 1)
                for ph, chunk, step in tails(phase, b, first, j):
                    par = parity(j, step)
                    bank = ps[:, tail_bank(par), :].rearrange("p (b c) -> p b c", c=C)
                    if (ph, step) == (DIFFUSE, 2):
                        dve.wait_ge(acc_turned, chunk + 1)
                        nc.vector.tensor_tensor(x[:, chunk], x[:, chunk], bank, ALU.add).then_inc(x1_ready, 1)
                        dve.wait_ge(x1_ready, chunk + 1)
                        ln_stats(CHUNKS + chunk, par, x[:, chunk])
                    if (ph, step) == (DIFFUSE, 3):
                        ln_newton(CHUNKS + chunk, par)
                        if not known_zero(chunk):
                            dve.wait_ge(h2_ready, chunk)
                        nc.vector.scalar_tensor_tensor(out=shift[:, par], in0=mv[:, par, :, 0], scalar=-1.0,
                                                       in1=rstd[:, par], op0=ALU.mult,
                                                       op1=ALU.mult).then_inc(shift_ready, 1)
                    if (ph, step, par) == (DIFFUSE, 5, 1):
                        k = strip_of(b, first)
                        dve.wait_ge(msg_summed, k + 1)
                        nc.vector.tensor_tensor(msg[:, bass.ds(k * TILES, TILES), :],
                                                ps[:, 4:6, :].rearrange("p a (t c) -> p (a t) c", c=C),
                                                b_sb[:, :].unsqueeze(1).broadcast_to([P, TILES, C]),
                                                ALU.add).then_inc(msg_ready, 1)
                    if (ph, step) == (MESSAGE, 5):
                        dve.wait_ge(acc_turned, CHUNKS + chunk + 1)
                        nc.vector.tensor_tensor(x[:, chunk], x[:, chunk], bank, ALU.add).then_inc(out_ready, 1)
                if phase == DIFFUSE:
                    for q in range(GROUPS):
                        diffuse_turn(b, first, j, q)
                    z_unit(phase, b, first, j)
                    mask_unit(phase, b, first, j)
                    return
                if phase == MESSAGE:
                    message_turn(b, first, j)
                mask_unit(phase, b, first, j)
                if phase != DRAIN:
                    mag_unit(phase, b, first, j)
                z_unit(phase, b, first, j)
                if phase == SPECTRUM and first:
                    for c in LN_IN.get(j, ()):
                        ln_x_stats(c)
                        ln_x_apply(c)
                if phase == SPECTRUM and first and j == 4:
                    dve.wait_ge(small_here, 16 * (STRIPS + 3))
                    nc.vector.tensor_scalar(t_neg[:, :], t_sb[:, :], T_MIN, -1.0, ALU.max, ALU.mult)\
                        .then_inc(t_ready, 1)

            ln_x_stats(0)
            ln_x_apply(0)
            bodies(dve, SPECTRUM, period)
            bodies(dve, DIFFUSE, period)
            bodies(dve, MESSAGE, period)
            bodies(dve, DRAIN, period, 7)

        @block.tensor
        def _(pe):
            def turn_unit(phase, b, first, j):
                if late(phase, first, j, 4) != SPECTRUM:
                    return
                jj = (j - 4) % BODY
                bb = b if j >= 4 else (BODIES - 1 if first else b - 1)
                pe.wait_ge(weight_done, BODY * bb + jj + 1)
                for t in range(TURNED):
                    n = TURNED * (BODY * bb + jj) + t
                    if not (isinstance(n, int) and n < 4):
                        pe.wait_ge(copied, n - 3)
                    for i in range(BLOCKS):
                        at = t * ROWS + i * P
                        last = nc.tensor.transpose(ps[:, turn_bank(jj, t), i * P:(i + 1) * P],
                                                   weight(SPECTRUM, jj % RING)[:, at:at + P], ident[:, :])
                    last.then_inc(turned, 1)

            def spectrum_period(phase, b, first, j):
                if first and j == 4:
                    pe.wait_ge(ident_ready, 2)
                if first and j == 5:
                    pe.wait_ge(small_here, 16 * (STRIPS + 3))
                    nc.tensor.transpose(ps[:, 2, 0:N // P], ev_rows[:, :], ident[0:N // P, 0:N // P])\
                        .then_inc(ev_transposed, 1)
                if not first or j > 0:
                    pe.wait_ge(unit_here[j % RING], 16 * (BODY // RING * b + j // RING + 1))
                turn_unit(phase, b, first, j)
                if first:
                    pe.wait_ge(h_ready, j + 1)
                elif j == 0:
                    pe.wait_ge(spec_copied, b)
                for i in range(BLOCKS):
                    if first and j == 0:
                        pe.wait_ge(first_here[i] if i < BLOCKS - 1 else unit_here[0], 16)
                    for half in range(2):
                        last = nc.tensor.matmul(ps[:, half, :], h[:, j, i, :],
                                                unit_full[:, j % RING, i, half * 512:(half + 1) * 512],
                                                start=(j == 0 and i == 0), stop=(j == BODY - 1 and i == BLOCKS - 1))
                last.then_inc(spectrum_used, 1)
                strip_tail(phase, b, first, j)

            def strip_tail(phase, b, first, j):
                strip = ended_strip(phase, b, first)
                if strip is None or j != 1:
                    return
                pe.wait_ge(spec_copied, strip + 1)
                pe.wait_ge(coef_ready, 1)
                for t in range(TILES):
                    last = nc.tensor.transpose(ps[:, 2 + t // 4, (t % 4) * P:(t % 4 + 1) * P],
                                               spec_t[:, t, :], ident[:, :])
                last.then_inc(spec_turned, 1)

            def diffuse_sum(b, first, j, q):
                u = BODY * b + j
                strip = j % STRIPS
                acc = j // STRIPS
                pe.wait_ge(diffuse_turned, GROUPS * u + q + 1)
                if q == 0 and first and j == 0:
                    pe.wait_ge(spec_copied, STRIPS)
                if q == 0 and first and j < STRIPS:
                    pe.wait_ge(s_ready, strip + 1)
                if q == 0 and strip == 0 and not first:
                    pe.wait_ge(acc_copied, 2 * b + acc - 1)
                for tile in (q, q + GROUPS):
                    last = nc.tensor.matmul(ps[:, acc, :], s[:, strip * TILES + tile, :], adj_t[:, j % 2, tile, :],
                                            start=(strip == 0 and tile == 0),
                                            stop=(strip == STRIPS - 1 and tile == TILES - 1))
                last.then_inc(diffuse_done, 1)

            def turn_acc(ph, chunk, bank):
                n = chunk + (CHUNKS if ph == MESSAGE else 0)
                pe.wait_ge(acc_copied, n + 1)
                for i in range(BLOCKS):
                    last = nc.tensor.transpose(ps[:, bank, i * P:(i + 1) * P], acc_t[:, i * P:(i + 1) * P],
                                               ident[:, :])
                last.then_inc(acc_turned, 1)

            def chunk_tails(phase, b, first, j):
                for ph, chunk, step in tails(phase, b, first, j):
                    par = parity(j, step)
                    bank = tail_bank(par)
                    if (ph, step) == (DIFFUSE, 1):
                        if first and ph == phase:
                            pe.wait_ge(s_ready, STRIPS)
                        turn_acc(ph, chunk, bank)
                    if (ph, step) == (DIFFUSE, 3):
                        pe.wait_ge(h2_ready, chunk + 1)
                        for i in range(BLOCKS):
                            last = nc.tensor.transpose(ps[:, bank, i * P:(i + 1) * P], h2[:, i], ident[:, :])
                        last.then_inc(h2_turned, 1)
                    if (ph, step, par) == (DIFFUSE, 4, 1):
                        k = strip_of(b, first)
                        pe.wait_ge(h2t_ready, chunk + 1)
                        if ph == phase and first:
                            pe.wait_ge(copied, TURNED * UNITS)
                        for t in range(TILES):
                            last = nc.tensor.matmul(ps[:, 4 + t // 4, (t % 4) * P:(t % 4 + 1) * P],
                                                    h2_t[:, t, :],
                                                    w_sb[:, :], start=True, stop=True)
                        last.then_inc(msg_summed, 1)
                    if (ph, step) == (MESSAGE, 4):
                        turn_acc(ph, chunk, bank)

            def diffuse_period(phase, b, first, j):
                turn_unit(phase, b, first, j)
                for q in range(GROUPS):
                    diffuse_sum(b, first, j, q)
                    if q == 1:
                        strip_tail(phase, b, first, j)
                        chunk_tails(phase, b, first, j)

            def stored_sum(bb, jj):
                strip, acc, slot = jj % STRIPS, jj // STRIPS, jj % RING
                start = isinstance(bb, int) and bb == 0
                if strip == 0 and start:
                    pe.wait_ge(acc_copied, CHUNKS - 1 + acc)
                elif strip == 0:
                    pe.wait_ge(acc_copied, CHUNKS + 2 * bb + acc - 1)
                if start and acc == 0:
                    pe.wait_ge(msg_ready, strip + 1)
                n_loads = 2 if n_stored(slot) > TILES - RAW else 1
                pe.wait_ge(w_here[slot], 16 * n_loads * (BODY // RING * bb + jj // RING + 1))
                for t in range(n_stored(slot)):
                    last = nc.tensor.matmul(ps[:, acc, :], msg[:, strip * TILES + t, :],
                                            w_back[:, slot, t, :] if t < TILES - RAW else w_back_last(slot),
                                            start=(strip == 0 and t == 0), stop=False)
                last.then_inc(stored_used[slot], 1)

            def message_sum(phase, b, first, j):
                if phase == MESSAGE and first:
                    if j in STORED_FIRST:
                        stored_sum(0, STORED_FIRST[j])
                elif late(phase, first, j, STORED_LAG) == MESSAGE:
                    stored_sum(*ago(b, first, j, STORED_LAG))
                if late(phase, first, j, MSG_LAG) != MESSAGE:
                    return
                g = count(phase, b, j) - MSG_LAG
                jj = (j - MSG_LAG) % BODY
                bb = b if j >= MSG_LAG else (BODIES - 1 if first else b - 1)
                strip, acc, slot = jj % STRIPS, jj // STRIPS, jj % RING
                pe.wait_ge(weight_done, g + 1)
                stored = n_stored(slot)
                for t in range(stored, TILES):
                    last = nc.tensor.matmul(ps[:, acc, :], msg[:, strip * TILES + t, :],
                                            by_tile(weight(MESSAGE, slot))[:, t - stored, :],
                                            start=False, stop=(strip == STRIPS - 1 and t == TILES - 1))
                last.then_inc(message_done, 1)

            def message_period(phase, b, first, j):
                message_sum(phase, b, first, j)
                chunk_tails(phase, b, first, j)

            bodies(pe, SPECTRUM, spectrum_period)
            bodies(pe, DIFFUSE, diffuse_period)
            bodies(pe, MESSAGE, message_period)
            bodies(pe, DRAIN, message_period, 7)


_INS = ["x", "adj", "L0_gnn_evals", "L0_gnn_t", "L1_gnn_W", "L1_gnn_B"]


def kernel(**inputs):
    import numpy as _np
    import concourse.bacc as _bacc
    from concourse import mybir as _mybir
    from concourse.bass_utils import run_bass_kernel_spmd as _run

    nc = _bacc.Bacc("TRN2", target_bir_lowering=False, num_devices=1)
    arrays, args = {}, []
    for name in _INS:
        a = _np.ascontiguousarray(inputs[name])
        arrays[f"in_{name}_dram"] = a
        args.append(nc.dram_tensor(f"in_{name}_dram", a.shape, _mybir.dt.from_np(a.dtype), kind="ExternalInput").ap())
    rows, cols = arrays["in_x_dram"].shape
    out = nc.dram_tensor("out_dram", (rows, cols), _mybir.dt.float32, kind="ExternalOutput").ap()
    adjacency_diffusion_message_kernel(nc, *args, out)
    r = _run(nc, [arrays], core_ids=[0])
    return r.results[0]["out_dram"]
```
